# Optimizing a Trainium2 kernel written in Bass

```python
import numpy as np
import jax
import jax.numpy as jnp

def _softmax(x, axis=-1):
    return jax.nn.softmax(x, axis=axis)

def _gelu(x):
    return jax.nn.gelu(x, approximate=True)

def _silu(x):
    return jax.nn.silu(x)

def _sigmoid(x):
    return jax.nn.sigmoid(x)

def _layernorm(x, axis=-1, eps=1e-05):
    m = jnp.mean(x, axis=axis, keepdims=True)
    v = jnp.var(x, axis=axis, keepdims=True)
    return (x - m) / jnp.sqrt(v + eps)

def _scatter_add(tgt, idx, src, axis=0):
    return tgt.at[idx].add(src)

def _segment_sum(src, seg, n):
    return jax.ops.segment_sum(src, seg, n)
kernel_name = 'mk_audio_tower_d1_tok_audfeat512_r4_d3d364'

def setup_inputs(seed: int=0):
    np.random.seed(seed)
    _w = jnp.asarray

    def _rec_inputs():
        import jax
        import jax.numpy as jnp
        _rk = jax.random.key(seed)
        x = -7.10856e-05 + 0.999911 * jax.random.normal(jax.random.fold_in(_rk, 1), (8, 375, 128), jnp.float32)
        return x
    x = _rec_inputs()

    def _L0_tok_setup():
        import jax, jax.numpy as jnp
        import numpy as np
        EPS = 1e-05

        def conv1d(x, w, b, stride=1, padding=0):
            out = jax.lax.conv_general_dilated(x, w, window_strides=(stride,), padding=[(padding, padding)], dimension_numbers=('NCH', 'OIH', 'NCH'))
            return out + b[None, :, None]

        def layer_norm(x, g, b):
            mu = jnp.mean(x, axis=-1, keepdims=True)
            var = jnp.mean(jnp.square(x - mu), axis=-1, keepdims=True)
            return (x - mu) * jax.lax.rsqrt(var + EPS) * g + b
        key = jax.random.key(seed)
        ks = jax.random.split(key, 16)
        B, T, H = (64, 512, 128)
        Bn = H // 2
        s = 0.02
        return {'x': jax.random.normal(ks[0], (B, T, H), dtype=jnp.float32), 'w_compress': jax.random.normal(ks[1], (Bn, H, 1), dtype=jnp.float32) * s, 'b_compress': jnp.zeros((Bn,), dtype=jnp.float32), 'w_main': jax.random.normal(ks[2], (Bn, Bn, 3), dtype=jnp.float32) * s, 'b_main': jnp.zeros((Bn,), dtype=jnp.float32), 'w_expand': jax.random.normal(ks[3], (H, Bn, 1), dtype=jnp.float32) * s, 'b_expand': jnp.zeros((H,), dtype=jnp.float32), 'g_conv_norm': jnp.ones((H,), dtype=jnp.float32), 'b_conv_norm': jnp.zeros((H,), dtype=jnp.float32), 'w_ff1': jax.random.normal(ks[4], (Bn, H), dtype=jnp.float32) * s, 'b_ff1': jnp.zeros((Bn,), dtype=jnp.float32), 'w_ff2': jax.random.normal(ks[5], (H, Bn), dtype=jnp.float32) * s, 'b_ff2': jnp.zeros((H,), dtype=jnp.float32), 'g_ff_norm': jnp.ones((H,), dtype=jnp.float32), 'b_ff_norm': jnp.zeros((H,), dtype=jnp.float32)}
    _L0_tok_all = _L0_tok_setup()
    _L0_tok_in = {k: v for k, v in _L0_tok_all.items() if k in ('w_compress', 'b_compress', 'w_main', 'b_main', 'w_expand', 'b_expand', 'g_conv_norm', 'b_conv_norm', 'w_ff1', 'b_ff1', 'w_ff2', 'b_ff2', 'g_ff_norm', 'b_ff_norm')}
    del _L0_tok_all

    def _L0_attn_setup():
        import jax, jax.numpy as jnp
        import numpy as np
        EMBED_DIM = 128
        key = jax.random.key(seed)
        k1, k2, k3 = jax.random.split(key, 3)
        B, T, E = (8, 512, EMBED_DIM)
        x = jax.random.normal(k1, (B, T, E), dtype=jnp.float32)
        Wq = jax.random.normal(k2, (E, E), dtype=jnp.float32) * E ** (-0.5)
        bq = jnp.zeros((E,), dtype=jnp.float32)
        Wk = jax.random.normal(k3, (E, E), dtype=jnp.float32) * E ** (-0.5)
        bk = jnp.zeros((E,), dtype=jnp.float32)
        return {'x': x, 'Wq': Wq, 'bq': bq, 'Wk': Wk, 'bk': bk}
    _L0_attn_all = _L0_attn_setup()
    _L0_attn_in = {k: v for k, v in _L0_attn_all.items() if k in ('Wq', 'bq', 'Wk', 'bk')}
    del _L0_attn_all

    def _L0_ffn_setup():
        import jax, jax.numpy as jnp
        import numpy as np
        E = 8
        TOP_K = 2
        D = 128
        H = 256
        B, S = (16, 1024)
        key = jax.random.key(seed)
        ks = jax.random.split(key, 10)
        sd = lambda fan_in: 1.0 / np.sqrt(fan_in)
        x = jax.random.normal(ks[0], (B, S, D), dtype=jnp.float32)
        gw1 = jax.random.uniform(ks[1], (D, D // 2), jnp.float32, -sd(D), sd(D))
        gb1 = jnp.zeros((D // 2,), jnp.float32)
        gw2 = jax.random.uniform(ks[2], (D // 2, E), jnp.float32, -sd(D // 2), sd(D // 2))
        gb2 = jnp.zeros((E,), jnp.float32)
        we1 = jax.random.uniform(ks[3], (E, D, H), jnp.float32, -sd(D), sd(D))
        be1 = jnp.zeros((E, H), jnp.float32)
        we2 = jax.random.uniform(ks[4], (E, H, D), jnp.float32, -sd(H), sd(H))
        be2 = jnp.zeros((E, D), jnp.float32)
        return {'x': x, 'gw1': gw1, 'gb1': gb1, 'gw2': gw2, 'gb2': gb2, 'we1': we1, 'be1': be1, 'we2': we2, 'be2': be2}
    _L0_ffn_all = _L0_ffn_setup()
    _L0_ffn_in = {k: v for k, v in _L0_ffn_all.items() if k in ('gw1', 'gb1', 'gw2', 'gb2', 'we1', 'be1', 'we2', 'be2')}
    del _L0_ffn_all
    return {'x': x, 'L0_tok_w_compress': _L0_tok_in['w_compress'], 'L0_tok_b_compress': _L0_tok_in['b_compress'], 'L0_tok_w_main': _L0_tok_in['w_main'], 'L0_tok_b_main': _L0_tok_in['b_main'], 'L0_tok_w_expand': _L0_tok_in['w_expand'], 'L0_tok_b_expand': _L0_tok_in['b_expand'], 'L0_tok_g_conv_norm': _L0_tok_in['g_conv_norm'], 'L0_tok_b_conv_norm': _L0_tok_in['b_conv_norm'], 'L0_tok_w_ff1': _L0_tok_in['w_ff1'], 'L0_tok_b_ff1': _L0_tok_in['b_ff1'], 'L0_tok_w_ff2': _L0_tok_in['w_ff2'], 'L0_tok_b_ff2': _L0_tok_in['b_ff2'], 'L0_tok_g_ff_norm': _L0_tok_in['g_ff_norm'], 'L0_tok_b_ff_norm': _L0_tok_in['b_ff_norm'], 'L0_attn_Wq': _L0_attn_in['Wq'], 'L0_attn_bq': _L0_attn_in['bq'], 'L0_attn_Wk': _L0_attn_in['Wk'], 'L0_attn_bk': _L0_attn_in['bk'], 'L0_ffn_gw1': _L0_ffn_in['gw1'], 'L0_ffn_gb1': _L0_ffn_in['gb1'], 'L0_ffn_gw2': _L0_ffn_in['gw2'], 'L0_ffn_gb2': _L0_ffn_in['gb2'], 'L0_ffn_we1': _L0_ffn_in['we1'], 'L0_ffn_be1': _L0_ffn_in['be1'], 'L0_ffn_we2': _L0_ffn_in['we2'], 'L0_ffn_be2': _L0_ffn_in['be2']}

def reference(x, L0_tok_w_compress, L0_tok_b_compress, L0_tok_w_main, L0_tok_b_main, L0_tok_w_expand, L0_tok_b_expand, L0_tok_g_conv_norm, L0_tok_b_conv_norm, L0_tok_w_ff1, L0_tok_b_ff1, L0_tok_w_ff2, L0_tok_b_ff2, L0_tok_g_ff_norm, L0_tok_b_ff_norm, L0_attn_Wq, L0_attn_bq, L0_attn_Wk, L0_attn_bk, L0_ffn_gw1, L0_ffn_gb1, L0_ffn_gw2, L0_ffn_gb2, L0_ffn_we1, L0_ffn_be1, L0_ffn_we2, L0_ffn_be2):
    import jax
    import jax.numpy as jnp

    def _L0_tok_ref(x, w_compress, b_compress, w_main, b_main, w_expand, b_expand, g_conv_norm, b_conv_norm, w_ff1, b_ff1, w_ff2, b_ff2, g_ff_norm, b_ff_norm):
        import jax, jax.numpy as jnp
        import numpy as np
        EPS = 1e-05

        def conv1d(x, w, b, stride=1, padding=0):
            out = jax.lax.conv_general_dilated(x, w, window_strides=(stride,), padding=[(padding, padding)], dimension_numbers=('NCH', 'OIH', 'NCH'))
            return out + b[None, :, None]

        def layer_norm(x, g, b):
            mu = jnp.mean(x, axis=-1, keepdims=True)
            var = jnp.mean(jnp.square(x - mu), axis=-1, keepdims=True)
            return (x - mu) * jax.lax.rsqrt(var + EPS) * g + b
        xt = jnp.transpose(x, (0, 2, 1))
        identity = xt
        h = jax.nn.silu(conv1d(xt, w_compress, b_compress))
        h = jax.nn.silu(conv1d(h, w_main, b_main, stride=1, padding=1))
        h = conv1d(h, w_expand, b_expand)
        h = jnp.transpose(h, (0, 2, 1))
        identity = jnp.transpose(identity, (0, 2, 1))
        y = layer_norm(h + identity, g_conv_norm, b_conv_norm)
        ff = jnp.einsum('bth,oh->bto', y, w_ff1) + b_ff1
        ff = jax.nn.gelu(ff, approximate=False)
        ff = jnp.einsum('bto,ho->bth', ff, w_ff2) + b_ff2
        y = layer_norm(ff + y, g_ff_norm, b_ff_norm)
        yt = jnp.transpose(y, (0, 2, 1))
        pooled = jax.lax.reduce_window(yt, -jnp.inf, jax.lax.max, (1, 1, 3), (1, 1, 1), 'VALID')
        return jnp.transpose(pooled, (0, 2, 1))

    def _L0_attn_ref(x, Wq, bq, Wk, bk):
        import jax, jax.numpy as jnp
        import numpy as np
        EMBED_DIM = 128
        scaling = jnp.float32(EMBED_DIM ** (-0.5))
        q = (x @ Wq + bq) * scaling
        k = x @ Wk + bk
        scores = jnp.einsum('bqe,bke->bqk', q, k)
        attn = jax.nn.softmax(scores, axis=-1)
        return jnp.einsum('bqk,bke->bqe', attn, x)

    def _L0_ffn_ref(x, gw1, gb1, gw2, gb2, we1, be1, we2, be2):
        import jax, jax.numpy as jnp
        import numpy as np
        E = 8
        TOP_K = 2
        D = 128
        H = 256
        B, S = (16, 1024)
        b, s, d = x.shape
        xf = x.reshape(-1, d)
        T = xf.shape[0]
        gate_logits = jax.nn.relu(xf @ gw1 + gb1) @ gw2 + gb2
        gate_weights = jax.nn.softmax(gate_logits, axis=-1)
        top_w, top_idx = jax.lax.top_k(gate_weights, TOP_K)
        top_w = jax.nn.softmax(top_w, axis=-1)
        combine = jnp.zeros((T, E), dtype=xf.dtype)
        combine = combine.at[jnp.arange(T)[:, None], top_idx].add(top_w)
        out = jnp.zeros_like(xf)
        for e in range(E):
            h = jax.nn.gelu(xf @ we1[e] + be1[e], approximate=False)
            y = h @ we2[e] + be2[e]
            out = out + combine[:, e:e + 1] * y
        return out.reshape(b, s, d)
    h = _L0_tok_ref(x, L0_tok_w_compress, L0_tok_b_compress, L0_tok_w_main, L0_tok_b_main, L0_tok_w_expand, L0_tok_b_expand, L0_tok_g_conv_norm, L0_tok_b_conv_norm, L0_tok_w_ff1, L0_tok_b_ff1, L0_tok_w_ff2, L0_tok_b_ff2, L0_tok_g_ff_norm, L0_tok_b_ff_norm)
    h = h + _L0_attn_ref(_layernorm(h, axis=-1), L0_attn_Wq, L0_attn_bq, L0_attn_Wk, L0_attn_bk)
    h = h + _L0_ffn_ref(_layernorm(h, axis=-1), L0_ffn_gw1, L0_ffn_gb1, L0_ffn_gw2, L0_ffn_gb2, L0_ffn_we1, L0_ffn_be1, L0_ffn_we2, L0_ffn_be2)
    return h

_drawn_inputs = setup_inputs


def setup_inputs(seed=0):
    import zlib

    import numpy as np

    out = dict(_drawn_inputs(seed))
    spreads = {'L0_tok_b_compress': (0.0, 0.8),
     'L0_tok_b_main': (0.0, 0.4),
     'L0_tok_b_expand': (0.0, 0.1),
     'L0_tok_g_conv_norm': (1.0, 0.2),
     'L0_tok_b_conv_norm': (0.0, 0.1),
     'L0_tok_b_ff1': (0.0, 0.374),
     'L0_tok_b_ff2': (0.0, 0.1),
     'L0_tok_g_ff_norm': (1.0, 0.2),
     'L0_tok_b_ff_norm': (0.0, 0.1),
     'L0_attn_bq': (0.0, 0.561),
     'L0_attn_bk': (0.0, 0.8),
     'L0_ffn_gb1': (0.0, 0.1),
     'L0_ffn_gb2': (0.0, 0.1),
     'L0_ffn_be1': (0.0, 0.429),
     'L0_ffn_be2': (0.0, 0.1)}
    factors = {'L0_tok_w_compress': 8.0, 'L0_tok_w_main': 6.467}
    for name, (base, spread) in spreads.items():
        noise = np.random.default_rng([zlib.crc32(name.encode()), seed]).standard_normal(out[name].shape)
        drawn = base * np.exp(spread * noise) if base else spread * noise
        out[name] = jnp.asarray(drawn.astype(out[name].dtype))
    for name, factor in factors.items():
        out[name] = (out[name] * factor).astype(out[name].dtype)
    return out
```

```python
from contextlib import ExitStack

import concourse.bass as bass
from concourse import mybir

B, T, D = 8, 375, 128
BN = 64
TP = T - 2
E, H = 8, 256
NJ = 3
P = T // NJ
ROWS = [len(range(j, TP, NJ)) for j in range(NJ)]
OFF = [sum(ROWS[:j]) for j in range(NJ)]
TE = TP + 1
HC = H // 128
NC = E * HC
KC = 72
EPS = 1e-5
SCALE = float(D) ** -0.5

LAG = {"a1": 0, "a2": 0, "a3": 0, "a3b": 0,
       "a4": 1, "a5": 1, "a6": 1, "a6b": 1,
       "s3a": 2, "s3b": 2, "b1": 2, "b2": 2,
       "sc": 3, "pt": 3, "at": 3, "atb": 3,
       "h1": 4, "g1": 4, "g2": 4, "g3": 4, "g4": 4,
       "moe": 5, "out": 6}
ORDER = [0, "s3a", "h1", 1, "g1", "out", 2, "a4", "a1", 3, "s3b", "g2", 4, "a5", "sc", 5, "a2", 6, "a6", 7,
         "pt", "b1", 8, "a6b", 9, "at", 10, "g3", "b2", 11, "a3", 12, "atb", 13, "g4", 14, "a3b", 15, "flush"]
STEPS = B + 6


def pieces(t):
    for name in ORDER:
        lag = LAG["moe" if name == "flush" or isinstance(name, int) else name]
        if 0 <= t - lag < B:
            yield name, t - lag


def audio_tower(nc, x, xt, wc, bc, wm, bm, we, be, g1, b1, wf1, bf1, wf2, bf2, g2, b2, wq, bq, wk, bk,
                gw1, gb1, gw2, gb2, we1, be1, we2, be2, out):
    fp32, fp32r, u32 = mybir.dt.float32, mybir.dt.float32r, mybir.dt.uint32
    ALU, ACT, AX = mybir.AluOpType, mybir.ActivationFunctionType, mybir.AxisListType

    with ExitStack() as ctx:
        def sb(name, shape, dt=fp32):
            return ctx.enter_context(nc.sbuf_tensor(name, shape, dt))

        def sem(name):
            return ctx.enter_context(nc.semaphore(name))

        x_sb = sb("x_sb", [P, B, NJ * D])
        xt_sb = sb("xt_sb", [D, B, T])
        wc_sb = sb("wc_sb", [D, BN])
        wm_sb = sb("wm_sb", [BN, 3, BN])
        we_sb = sb("we_sb", [BN, D])
        wf1_sb = sb("wf1_sb", [D, BN])
        wf2_sb = sb("wf2_sb", [BN, D])
        wq_sb = sb("wq_sb", [D, D])
        wk_sb = sb("wk_sb", [D, D])
        gw1_sb = sb("gw1_sb", [D, BN])
        gw2_sb = sb("gw2_sb", [BN, E])
        bias64 = sb("bias64", [BN, 8])
        bias128 = sb("bias128", [D, 2 + NC])
        rows = sb("rows", [P, 6, D])
        gb2_sb = sb("gb2_sb", [P, NJ, E])
        w1_sb = sb("w1_sb", [D, E, H])
        w1hi = sb("w1hi", [D, E, H], fp32r)
        w1lo = sb("w1lo", [D, E, H], fp32r)
        w2_sb = sb("w2_sb", [128, NC, D])
        be2_sb = sb("be2_sb", [KC, D])
        be2hi = sb("be2hi", [KC, D], fp32r)
        ident = sb("ident", [128, 128])
        sel32 = sb("sel32", [KC, E, D])
        sel = sb("sel", [KC, E, D], fp32r)
        iota_e = sb("iota_e", [P, NJ, E])
        mhalf = sb("mhalf", [P, NJ])

        th1, z1 = sb("th1", [BN, T]), sb("z1", [BN, T])
        th2, z2 = sb("th2", [BN, T]), sb("z2", [BN, T])
        hc1 = sb("hc1", [BN, T + 2])
        hc2 = sb("hc2", [BN, T])
        r1 = sb("r1", [P, NJ, D])
        n1 = sb("n1", [P, NJ, D])
        y = sb("y", [P, NJ, D])
        yb = sb("yb", [P, NJ, D])
        y_t = sb("y_t", [D, T])
        f1 = sb("f1", [BN, T])
        r2 = sb("r2", [P, NJ, D])
        n2 = sb("n2", [P, NJ, D])
        y2 = sb("y2", [P, NJ, D])
        y2next = sb("y2next", [P, 2, D])
        m12 = sb("m12", [P, D])
        m01 = sb("m01", [P, D])
        h = sb("h", [P, B, NJ * D])
        xn3 = sb("xn3", [P, NJ, D])
        xn3v = sb("xn3v", [P, B, NJ * D])
        xn_t = sb("xn_t", [D, TP])
        q_t = sb("q_t", [D, TE])
        k_t = sb("k_t", [D, TP])
        nmax = sb("nmax", [P, NJ])
        prob = sb("prob", [P, NJ, TP])
        psum_row = sb("psum_row", [P, NJ])
        rinv = sb("rinv", [P, NJ])
        prob_t = sb("prob_t", [P, NJ, TE])
        h2 = sb("h2", [P, B, NJ * D])
        xn4 = sb("xn4", [P, NJ, D])
        x32 = sb("x32", [D, TP])
        xhi = sb("xhi", [D, B, TE], fp32r)
        xlo = sb("xlo", [D, B, TE], fp32r)
        gh_t = sb("gh_t", [BN, TE])
        lg = sb("lg", [P, NJ, E])
        lmax = sb("lmax", [P, NJ])
        le = sb("le", [P, NJ, E])
        ge = sb("ge", [P, NJ, E])
        gsum = sb("gsum", [P, NJ])
        grec = sb("grec", [P, NJ])
        gp = sb("gp", [P, NJ, E])
        top = sb("top", [P, NJ, 8])
        topi = sb("topi", [P, NJ, 8], u32)
        topf = sb("topf", [P, NJ, 2])
        dd = sb("dd", [P, NJ])
        th3 = sb("th3", [P, NJ])
        w_top = sb("w_top", [P, 2, NJ])
        one1, one2 = sb("one1", [P, NJ, E]), sb("one2", [P, NJ, E])
        s1, s2 = sb("s1", [P, NJ, E]), sb("s2", [P, NJ, E])
        comb = sb("comb", [P, NJ, E])
        chi = sb("chi", [P, NJ, E], fp32r)
        c3 = sb("c3", [P, NJ, KC])
        c_t = sb("c_t", [KC, B, TE], fp32r)
        g_sb = [sb(f"g_sb{i}", [128, TP]) for i in range(2)]
        gs_sb = [sb(f"gs_sb{i}", [128, TP]) for i in range(4)]
        yo = sb("yo", [D, TE])
        ob = sb("ob", [P, NJ * D])
        stat = [sb(f"stat{i}", [P, NJ, 6]) for i in range(4)]
        mv = [sb(f"mv{i}", [P, NJ, 2]) for i in range(4)]
        ve = [sb(f"ve{i}", [P, NJ]) for i in range(4)]
        rstd = [sb(f"rstd{i}", [P, NJ]) for i in range(4)]

        def bank(name):
            return ctx.enter_context(nc.psum_tensor(name, [128, 512], fp32))

        F = [bank(f"F{i}") for i in range(3)]
        PH = [bank(f"PH{i}") for i in range(2)]
        CB = [bank(f"CB{i}") for i in range(2)]
        PY = bank("PY")

        names = """rows wearly wmid wlate xb ident init init2 wsplit
            h1 x32 xs g1 gh g2 le ge g3 dd th3 c3 g4 ct
            a1 z1 hc1 a2 z2 hc2 a3 y yb a4 yt a5 f1 a6 y2 shift xn3 xnv b1 xnt qp kp q k
            sc nmax prob pt pta ptd at xn4 cb l1 gl gs l2 yo ot ob out dve act""".split()
        S = {n: sem("s_" + n) for n in names}
        s_x = [sem(f"s_x{b}") for b in range(B)]
        s_xt = [sem(f"s_xt{b}") for b in range(B)]
        s_ve = [sem(f"s_ve{i}") for i in range(4)]
        S |= {f"ve{i}": s_ve[i] for i in range(4)}
        s_rstd = [sem(f"s_rstd{i}") for i in range(4)]

        def wait(eng, name, value):
            if value > 0:
                eng.wait_ge(S[name], value)

        block = ctx.enter_context(nc.Block())

        @block.sync
        def _(sp):
            sp.dma_start(wc_sb[:], wc).then_inc(S["wearly"], 16)
            sp.dma_start(wm_sb[:], wm).then_inc(S["wearly"], 16)
            sp.dma_start(we_sb[:], we).then_inc(S["wearly"], 16)
            for b in range(B):
                sp.dma_start(xt_sb[:, b, :], xt[:, b, :]).then_inc(s_xt[b], 16)
                sp.dma_start(x_sb[:, b, :], x[b].rearrange("(p j) d -> p (j d)", j=NJ)).then_inc(s_x[b], 16)
            sp.dma_start(w1_sb[:], we1.rearrange("e d h -> d e h")).then_inc(S["wlate"], 16)
            sp.dma_start(w2_sb[:], we2.rearrange("e (c p) d -> p (e c) d", p=128)).then_inc(S["wlate"], 16)
            for t in range(STEPS + 1):
                for name, n in pieces(t):
                    if name == "a6b":
                        wait(sp, "y2", n + 1)
                        sp.dma_start(y2next[0:P - 1, :, :], y2[1:P, 0:2, :]).then_inc(S["shift"], 16)
                    if name == "out":
                        wait(sp, "ob", n + 1)
                        sp.dma_start(out[n, 0:TP - 1, :].rearrange("(p j) d -> p (j d)", j=NJ),
                                     ob[0:P - 1, :]).then_inc(S["out"], 16)
                        sp.dma_start(out[n, TP - 1:TP, :], ob[P - 1:P, 0:D]).then_inc(S["out"], 16)
            sp.wait_ge(S["out"], 32 * B)

        def pool_piece(pool, name, n):
            ln = {"a3": 0, "a6": 1, "s3a": 2, "at": 3}.get(name)
            if ln is not None:
                pool.wait_ge(s_ve[ln], n + 1)
                pool.tensor_tensor(rstd[ln][:], ve[ln][:], mhalf[:], ALU.pow).then_inc(s_rstd[ln], 1)
            if name == "a3b":
                wait(pool, "y", n + 1)
                pool.tensor_tensor(yb[:], y[:], rows[:, 3:4, :].broadcast_to([P, NJ, D]), ALU.add)\
                    .then_inc(S["yb"], 1)

        @block.gpsimd
        def _(pool):
            pool.memset(ident[:], 0.0).then_inc(S["ident"], 1)
            pool.memset(sel32[:], 0.0).then_inc(S["ident"], 1)
            pool.wait_ge(S["ident"], 2)
            pool.affine_select(out=ident[:], in_=ident[:], compare_op=ALU.not_equal, fill=1.0, base=0,
                               pattern=[[-1, 128]], channel_multiplier=1).then_inc(S["ident"], 1)
            for i, r in enumerate((0, 32)):
                pool.wait_ge(S["ident"], 3 + i)
                v = sel32[r:r + E, :, :]
                pool.affine_select(out=v, in_=v, compare_op=ALU.not_equal, fill=1.0, base=0,
                                   pattern=[[-1, E], [0, D]], channel_multiplier=1).then_inc(S["ident"], 1)
            pool.wait_ge(S["ident"], 5)
            pool.iota(iota_e[:], [[0, NJ], [1, E]], base=0, channel_multiplier=0,
                      allow_small_or_imprecise_dtypes=True).then_inc(S["init"], 1)
            pool.memset(mhalf[:], -0.5).then_inc(S["init"], 1)
            for v in (hc1[:, 0:1], hc1[:, T + 1:T + 2], q_t[:, TP:TE], prob_t[:, :, TP:TE], gh_t[:, TP:TE],
                      yo[:, TP:TE], y2next[:], c3[:], be2_sb[:]):
                pool.memset(v, 0.0).then_inc(S["init"], 1)
            for v in (xhi[:, :, TP:TE], xlo[:, :, TP:TE], c_t[:, :, TP:TE]):
                pool.memset(v.bitcast(fp32), 0.0).then_inc(S["init"], 1)
            pool.wait_ge(S["rows"], 16 * 6)
            for b in range(B):
                pool.wait_ge(s_x[b], 16)
                v = x_sb[:, b, :].rearrange("p (j d) -> p j d", j=NJ)
                pool.tensor_tensor(v, v, rows[:, 0:1, :].broadcast_to([P, NJ, D]), ALU.add).then_inc(S["xb"], 1)
                if b == 0:
                    first = list(pieces(0))
                    for name, n in first:
                        pool_piece(pool, name, n)
            pool.wait_ge(S["wsplit"], 1)
            pool.tensor_tensor(w1lo[:], w1_sb[:], w1hi[:].bitcast(fp32), ALU.subtract).then_inc(S["wsplit"], 1)
            for t in range(1, STEPS + 1):
                for name, n in pieces(t):
                    pool_piece(pool, name, n)

        @block.scalar
        def _(act):
            for i, b in enumerate((bc, bm, bf1, gb1)):
                act.dma_start(bias64[:, i:i + 1], b).then_inc(S["wearly"], 16)
            for i, b in enumerate((be, g1, b1, bf2, g2, b2)):
                act.dma_start(rows[:, i, :], b.broadcast_to([P, D])).then_inc(S["rows"], 16)
            for dst, src in ((wf1_sb[:], wf1), (wf2_sb[:], wf2), (wq_sb[:], wq), (wk_sb[:], wk), (gw1_sb[:], gw1),
                             (gw2_sb[:], gw2), (bias128[:, 0:1], bq), (bias128[:, 1:2], bk),
                             (bias128[:, 2:2 + NC], be1)):
                act.dma_start(dst, src).then_inc(S["wmid"], 16)
            for j in range(NJ):
                act.dma_start(gb2_sb[:, j, :], gb2.broadcast_to([P, E])).then_inc(S["wmid"], 16)
            act.wait_ge(S["init"], 14)
            for r in (0, 32, 64):
                act.dma_start(be2_sb[r:r + E, :], be2).then_inc(S["wlate"], 16)
            act.wait_ge(S["wearly"], 16 * 7)
            act.activation(bias64[:, 4:6], bias64[:, 0:2], ACT.Copy, scale=0.5).then_inc(S["act"], 1)
            act.wait_ge(S["act"], 1)

            for t in range(STEPS + 1):
                for name, n in pieces(t):
                    if name == "a1":
                        wait(act, "a1", n + 1)
                        wait(act, "hc1", n)
                        act.activation(th1[:], F[0][0:BN, 0:T], ACT.Tanh, bias=bias64[:, 4:5], scale=0.5)
                        act.activation(z1[:], F[0][0:BN, 0:T], ACT.Identity, bias=bias64[:, 4:5], scale=0.5)\
                            .then_inc(S["z1"], 1)
                    if name == "a2":
                        wait(act, "a2", n + 1)
                        wait(act, "hc2", n)
                        act.activation(th2[:], F[0][0:BN, 0:T], ACT.Tanh, bias=bias64[:, 5:6], scale=0.5)
                        act.activation(z2[:], F[0][0:BN, 0:T], ACT.Identity, bias=bias64[:, 5:6], scale=0.5)\
                            .then_inc(S["z2"], 1)
                    if name == "a4":
                        wait(act, "a4", n + 1)
                        if n == 0:
                            act.wait_ge(S["wmid"], 16 * 12)
                        act.activation(y_t[:], F[2][:, 0:T], ACT.Copy).then_inc(S["yt"], 1)
                    if name == "a5":
                        wait(act, "a5", n + 1)
                        act.activation(f1[:], F[2][0:BN, 0:T], ACT.Gelu, bias=bias64[:, 2:3]).then_inc(S["f1"], 1)
                    if name == "s3a" and n == 0:
                        act.wait_ge(S["wlate"], 16 * 5)
                        act.activation(w1hi[:], w1_sb[:], ACT.Copy).then_inc(S["wsplit"], 1)
                    if name == "b1":
                        wait(act, "xn3", n + 1)
                        act.activation(xn3v[:, n, :], xn3[:].rearrange("p j d -> p (j d)"), ACT.Copy)\
                            .then_inc(S["xnv"], 1)
                        wait(act, "b1", n + 1)
                        act.activation(xn_t[:], F[2][:, 0:TP], ACT.Copy).then_inc(S["xnt"], 1)
                    if name == "b2":
                        wait(act, "kp", n + 1)
                        act.activation(k_t[:], F[2][:, 0:TP], ACT.Identity, bias=bias128[:, 1:2])\
                            .then_inc(S["k"], 1)
                    if name == "sc":
                        for j in range(NJ):
                            wait(act, "nmax", NJ * n + j + 1)
                            act.activation(prob[:, j, :], F[j][0:P, 0:TP], ACT.Exp, bias=nmax[:, j:j + 1],
                                           accum_out=psum_row[:, j:j + 1]).then_inc(S["prob"], 1)
                    if name == "g2":
                        wait(act, "le", n + 1)
                        act.activation(ge[:], le[:], ACT.Exp).then_inc(S["ge"], 1)
                    if name == "pt":
                        for c in (0, 2):
                            wait(act, "pt", NJ * n + c + 1)
                            act.activation(prob_t[0:ROWS[c], c, 0:TP], F[c][0:ROWS[c], 0:TP], ACT.Copy)\
                                .then_inc(S["pta"], 1)
                    if name == "h1":
                        wait(act, "h1", n + 1)
                        wait(act, "xs", n)
                        act.activation(x32[:], F[0][:, 0:TP], ACT.Copy).then_inc(S["x32"], 1)
                    if name == "g1":
                        wait(act, "g1", n + 1)
                        act.activation(gh_t[:, 0:TP], F[1][0:BN, 0:TP], ACT.Relu, bias=bias64[:, 3:4])\
                            .then_inc(S["gh"], 1)
                    if name == "g3":
                        wait(act, "dd", n + 1)
                        act.activation(th3[:], dd[:], ACT.Tanh, scale=0.5).then_inc(S["th3"], 1)
                    if name == "g4":
                        wait(act, "g4", n + 1)
                        act.activation(c_t[:, n, 0:TP], F[1][0:KC, 0:TP], ACT.Copy).then_inc(S["ct"], 1)
                    if isinstance(name, int):
                        k = name
                        wait(act, "l1", NC * n + k + 1)
                        wait(act, "gs", NC * n + k - 1)
                        act.activation(g_sb[k % 2][:], PH[k % 2][:, 0:TP], ACT.Gelu, bias=bias128[:, 2 + k:3 + k])\
                            .then_inc(S["gl"], 1)
                    if name == "flush":
                        wait(act, "l2", NC * (n + 1))
                        wait(act, "ot", n)
                        act.activation(yo[:, 0:TP], PY[:, 0:TP], ACT.Copy).then_inc(S["yo"], 1)

        @block.vector
        def _(dve):
            chain = [0]

            def link(ins):
                chain[0] += 1
                ins.then_inc(S["dve"], 1)
                dve.wait_ge(S["dve"], chain[0])

            def bc(ap):
                return ap.broadcast_to([P, NJ, E])

            def ln_stats(i, src):
                for j in range(NJ):
                    last = dve.bn_stats(stat[i][:, j, :], src[j])
                link(last)
                for j in range(NJ):
                    last = dve.bn_aggr(mv[i][:, j, :], stat[i][:, j, :])
                link(last)
                dve.tensor_scalar(ve[i][:], mv[i][:, :, 1], EPS, None, ALU.add).then_inc(s_ve[i], 1)

            def ln_apply(i, n, src, dst):
                dve.wait_ge(s_rstd[i], n + 1)
                for j in range(NJ):
                    last = dve.tensor_scalar(dst[j], src[j], mv[i][:, j, 0:1], rstd[i][:, j:j + 1],
                                             ALU.subtract, ALU.mult)
                return last

            def tiles(ap):
                return [ap[:, j, :] for j in range(NJ)]

            def flat_tiles(ap, n):
                return [ap[:, n, j * D:(j + 1) * D] for j in range(NJ)]

            def row(i):
                return rows[:, i:i + 1, :].broadcast_to([P, NJ, D])

            dve.wait_ge(S["ident"], 5)
            dve.tensor_copy(sel[:], sel32[:]).then_inc(S["init2"], 1)
            dve.wait_ge(S["wlate"], 16 * 5)
            link(dve.tensor_copy(be2hi[:], be2_sb[:]))
            link(dve.tensor_tensor(be2_sb[64:KC, :], be2_sb[64:KC, :], be2hi[64:KC, :].bitcast(fp32), ALU.subtract))
            dve.tensor_copy(be2hi[64:KC, :], be2_sb[64:KC, :]).then_inc(S["init2"], 1)

            for t in range(STEPS + 1):
                for name, n in pieces(t):
                    if name == "a1":
                        wait(dve, "z1", n + 1)
                        if n == 0:
                            dve.wait_ge(S["init"], 14)
                        dve.scalar_tensor_tensor(hc1[:, 1:T + 1], th1[:], 1.0, z1[:], ALU.add, ALU.mult)\
                            .then_inc(S["hc1"], 1)
                    if name == "a2":
                        wait(dve, "z2", n + 1)
                        dve.scalar_tensor_tensor(hc2[:], th2[:], 1.0, z2[:], ALU.add, ALU.mult)\
                            .then_inc(S["hc2"], 1)
                    if name == "a3":
                        wait(dve, "a3", n + 1)
                        wait(dve, "xb", n + 1)
                        link(dve.tensor_tensor(r1[:].rearrange("p j d -> p (j d)"), F[0][0:P, 0:NJ * D],
                                               x_sb[:, n, :], ALU.add))
                        ln_stats(0, tiles(r1))
                    if name == "a3b":
                        link(ln_apply(0, n, tiles(r1), tiles(n1)))
                        link(dve.tensor_tensor(n1[:], n1[:], row(1), ALU.mult))
                        wait(dve, "a4", n)
                        wait(dve, "yb", n)
                        dve.tensor_tensor(y[:], n1[:], row(2), ALU.add).then_inc(S["y"], 1)
                    if name == "a6":
                        wait(dve, "a6", n + 1)
                        wait(dve, "yb", n + 1)
                        link(dve.tensor_tensor(r2[:].rearrange("p j d -> p (j d)"), F[1][0:P, 0:NJ * D],
                                               yb[:].rearrange("p j d -> p (j d)"), ALU.add))
                        ln_stats(1, tiles(r2))
                    if name == "a6b":
                        link(ln_apply(1, n, tiles(r2), tiles(n2)))
                        link(dve.tensor_tensor(n2[:], n2[:], row(4), ALU.mult))
                        dve.tensor_tensor(y2[:], n2[:], row(5), ALU.add).then_inc(S["y2"], 1)
                    if name == "s3a":
                        wait(dve, "y2", n + 1)
                        wait(dve, "shift", 16 * (n + 1))
                        hn = flat_tiles(h, n)
                        dve.tensor_tensor(m12[:], y2[:, 1, :], y2[:, 2, :], ALU.max)
                        link(dve.tensor_tensor(m01[:], y2next[:, 0, :], y2next[:, 1, :], ALU.max))
                        dve.tensor_tensor(hn[0], y2[:, 0, :], m12[:], ALU.max)
                        dve.tensor_tensor(hn[1], m12[:], y2next[:, 0, :], ALU.max)
                        link(dve.tensor_tensor(hn[2], y2[:, 2, :], m01[:], ALU.max))
                        ln_stats(2, hn)
                    if name == "s3b":
                        wait(dve, "b1", n)
                        wait(dve, "xnv", n)
                        ln_apply(2, n, flat_tiles(h, n), tiles(xn3)).then_inc(S["xn3"], 1)
                    if name == "b2":
                        wait(dve, "qp", n + 1)
                        dve.tensor_scalar(q_t[:, 0:TP], F[1][:, 0:TP], bias128[:, 0:1], SCALE, ALU.add, ALU.mult)\
                            .then_inc(S["q"], 1)
                    if name == "sc":
                        for j in range(NJ):
                            wait(dve, "sc", NJ * n + j + 1)
                            dve.tensor_reduce(nmax[:, j:j + 1], F[j][0:P, 0:TP], AX.X, ALU.max, negate=True)\
                                .then_inc(S["nmax"], 1)
                    if name == "pt":
                        wait(dve, "pt", NJ * n + 2)
                        dve.tensor_copy(prob_t[0:ROWS[1], 1, 0:TP], F[1][0:ROWS[1], 0:TP]).then_inc(S["ptd"], 1)
                    if name == "at":
                        wait(dve, "prob", NJ * (n + 1))
                        link(dve.reciprocal(rinv[:], psum_row[:]))
                        wait(dve, "at", n + 1)
                        for j in range(NJ):
                            last = dve.scalar_tensor_tensor(flat_tiles(h2, n)[j], F[0][0:P, j * D:(j + 1) * D],
                                                            rinv[:, j:j + 1], flat_tiles(h, n)[j], ALU.mult, ALU.add)
                        link(last)
                        ln_stats(3, flat_tiles(h2, n))
                    if name == "atb":
                        wait(dve, "h1", n)
                        ln_apply(3, n, flat_tiles(h2, n), tiles(xn4)).then_inc(S["xn4"], 1)
                    if name == "h1":
                        wait(dve, "x32", n + 1)
                        link(dve.tensor_copy(xhi[:, n, 0:TP], x32[:]))
                        dve.tensor_tensor(xlo[:, n, 0:TP], x32[:], xhi[:, n, 0:TP].bitcast(fp32), ALU.subtract)\
                            .then_inc(S["xs"], 1)
                    if name == "g2":
                        wait(dve, "g2", n + 1)
                        link(dve.tensor_tensor(lg[:], F[2][0:P, 0:NJ * E].rearrange("p (j e) -> p j e", j=NJ),
                                               gb2_sb[:], ALU.add))
                        link(dve.tensor_reduce(lmax[:], lg[:], AX.X, ALU.max))
                        dve.tensor_tensor(le[:], lg[:], bc(lmax[:].unsqueeze(2)), ALU.subtract).then_inc(S["le"], 1)
                    if name == "g3":
                        wait(dve, "ge", n + 1)
                        link(dve.tensor_reduce(gsum[:], ge[:], AX.X, ALU.add))
                        link(dve.reciprocal(grec[:], gsum[:]))
                        link(dve.tensor_tensor(gp[:], ge[:], bc(grec[:].unsqueeze(2)), ALU.mult))
                        for j in range(NJ):
                            last = dve.max(top[:, j, :], gp[:, j, :])
                        link(last)
                        dve.tensor_tensor(dd[:], top[:, :, 1], top[:, :, 0], ALU.subtract).then_inc(S["dd"], 1)
                        for j in range(NJ):
                            last = dve.max_index(topi[:, j, :], top[:, j, :], gp[:, j, :])
                        link(last)
                        link(dve.tensor_copy(topf[:], topi[:, :, 0:2]))
                        dve.tensor_tensor(one1[:], iota_e[:], bc(topf[:, :, 0:1]), ALU.is_equal)
                        dve.tensor_tensor(one2[:], iota_e[:], bc(topf[:, :, 1:2]), ALU.is_equal)
                        wait(dve, "th3", n + 1)
                        dve.tensor_scalar(w_top[:, 0, :], th3[:], -0.5, 0.5, ALU.mult, ALU.add)
                        link(dve.tensor_scalar(w_top[:, 1, :], th3[:], 0.5, 0.5, ALU.mult, ALU.add))
                        dve.tensor_tensor(s1[:], one1[:], bc(w_top[:, 0, :].unsqueeze(2)), ALU.mult)
                        link(dve.tensor_tensor(s2[:], one2[:], bc(w_top[:, 1, :].unsqueeze(2)), ALU.mult))
                        link(dve.tensor_tensor(comb[:], s1[:], s2[:], ALU.add))
                        link(dve.tensor_copy(chi[:], comb[:]))
                        wait(dve, "g4", n)
                        dve.tensor_copy(c3[:, :, 0:E], chi[:].bitcast(fp32))
                        dve.tensor_copy(c3[:, :, 64:64 + E], chi[:].bitcast(fp32))
                        dve.tensor_tensor(c3[:, :, 32:32 + E], comb[:], chi[:].bitcast(fp32), ALU.subtract)\
                            .then_inc(S["c3"], 1)
                    if isinstance(name, int):
                        k = name
                        wait(dve, "gl", NC * n + k + 1)
                        wait(dve, "cb", E * n + k // HC + 1)
                        wait(dve, "l2", NC * n + k - 3)
                        dve.tensor_tensor(gs_sb[k % 4][:], g_sb[k % 2][:], CB[k // HC % 2][:, 0:TP], ALU.mult)\
                            .then_inc(S["gs"], 1)
                    if name == "out":
                        wait(dve, "ot", n + 1)
                        wait(dve, "out", 32 * n)
                        dve.tensor_tensor(ob[:], F[2][0:P, 0:NJ * D], h2[:, n, :], ALU.add).then_inc(S["ob"], 1)

        @block.tensor
        def _(pe):
            reader = [None] * 3

            def claim(f, name, value):
                if reader[f]:
                    wait(pe, *reader[f])
                reader[f] = (name, value)
                return F[f]

            def transposes(dst, src, rows_of, off, width=D):
                for j in range(NJ):
                    last = pe.transpose(dst[0:width, off[j]:off[j] + rows_of[j]], src[0:rows_of[j], j, 0:width],
                                        ident[0:rows_of[j], 0:rows_of[j]])
                return last

            def second_layer(n, k):
                wait(pe, "gs", NC * n + k + 1)
                pe.matmul(PY[:, 0:TP], w2_sb[:, k, :], gs_sb[k % 4][:], start=False, stop=(k == NC - 1))\
                    .then_inc(S["l2"], 1)

            pe.wait_ge(S["ident"], 5)
            pe.wait_ge(S["wearly"], 16 * 7)
            for t in range(STEPS + 1):
                for name, n in pieces(t):
                    if name == "a1":
                        pe.wait_ge(s_xt[n], 16)
                        f = claim(0, "z1", n + 1)
                        pe.matmul(f[0:BN, 0:T], wc_sb[:], xt_sb[:, n, :], start=True, stop=True).then_inc(S["a1"], 1)
                    if name == "a2":
                        wait(pe, "hc1", n + 1)
                        f = claim(0, "z2", n + 1)
                        for k in range(3):
                            last = pe.matmul(f[0:BN, 0:T], wm_sb[:, k, :], hc1[:, k:k + T],
                                             start=(k == 0), stop=(k == 2))
                        last.then_inc(S["a2"], 1)
                    if name == "a3":
                        wait(pe, "hc2", n + 1)
                        f = claim(0, "ve0", n + 1)
                        for j in range(NJ):
                            last = pe.matmul(f[0:P, j * D:(j + 1) * D], hc2[:, j:T:NJ], we_sb[:],
                                             start=True, stop=True)
                        last.then_inc(S["a3"], 1)
                    if name == "a4":
                        wait(pe, "y", n + 1)
                        f = claim(2, "yt", n + 1)
                        transposes(f, y, [P] * NJ, [P * j for j in range(NJ)]).then_inc(S["a4"], 1)
                    if name == "a5":
                        wait(pe, "yt", n + 1)
                        if n == 0:
                            pe.wait_ge(S["wmid"], 16 * 12)
                        f = claim(2, "f1", n + 1)
                        pe.matmul(f[0:BN, 0:T], wf1_sb[:], y_t[:], start=True, stop=True).then_inc(S["a5"], 1)
                    if name == "a6":
                        wait(pe, "f1", n + 1)
                        f = claim(1, "ve1", n + 1)
                        for j in range(NJ):
                            last = pe.matmul(f[0:P, j * D:(j + 1) * D], f1[:, j * P:(j + 1) * P], wf2_sb[:],
                                             start=True, stop=True)
                        last.then_inc(S["a6"], 1)
                    if name == "b1":
                        wait(pe, "xn3", n + 1)
                        f = claim(2, "xnt", n + 1)
                        transposes(f, xn3, ROWS, OFF).then_inc(S["b1"], 1)
                    if name == "b2":
                        wait(pe, "xnt", n + 1)
                        f = claim(1, "q", n + 1)
                        pe.matmul(f[:, 0:TP], wq_sb[:], xn_t[:], start=True, stop=True).then_inc(S["qp"], 1)
                        f = claim(2, "k", n + 1)
                        pe.matmul(f[:, 0:TP], wk_sb[:], xn_t[:], start=True, stop=True).then_inc(S["kp"], 1)
                    if name == "sc":
                        wait(pe, "q", n + 1)
                        wait(pe, "k", n + 1)
                        for j in range(NJ):
                            f = claim(j, "prob", NJ * n + j + 1)
                            pe.matmul(f[0:P, 0:TP], q_t[:, OFF[j]:OFF[j] + P], k_t[:], start=True, stop=True)\
                                .then_inc(S["sc"], 1)
                    if name == "pt":
                        wait(pe, "prob", NJ * (n + 1))
                        for c in range(NJ):
                            f = claim(c, *(("ptd", n + 1) if c == 1 else ("pta", 2 * n + c // 2 + 1)))
                            for j in range(NJ):
                                last = pe.transpose(f[0:ROWS[c], OFF[j]:OFF[j] + ROWS[j]],
                                                    prob[0:ROWS[j], j, OFF[c]:OFF[c] + ROWS[c]],
                                                    ident[0:ROWS[j], 0:ROWS[j]])
                            last.then_inc(S["pt"], 1)
                    if name == "at":
                        wait(pe, "pta", 2 * (n + 1))
                        wait(pe, "ptd", n + 1)
                        wait(pe, "xnv", n + 1)
                        f = claim(0, "ve3", n + 1)
                        for j in range(NJ):
                            for c in range(NJ):
                                last = pe.matmul(f[0:P, j * D:(j + 1) * D],
                                                 prob_t[0:ROWS[c], c, OFF[j]:OFF[j] + P],
                                                 xn3v[0:ROWS[c], n, c * D:(c + 1) * D],
                                                 start=(c == 0), stop=(c == NJ - 1))
                        last.then_inc(S["at"], 1)
                    if name == "h1":
                        wait(pe, "xn4", n + 1)
                        f = claim(0, "x32", n + 1)
                        transposes(f, xn4, ROWS, OFF).then_inc(S["h1"], 1)
                    if name == "g1":
                        wait(pe, "x32", n + 1)
                        f = claim(1, "gh", n + 1)
                        pe.matmul(f[0:BN, 0:TP], gw1_sb[:], x32[:], start=True, stop=True).then_inc(S["g1"], 1)
                    if name == "g2":
                        wait(pe, "gh", n + 1)
                        f = claim(2, "le", n + 1)
                        for j in range(NJ):
                            last = pe.matmul(f[0:P, j * E:(j + 1) * E], gh_t[:, OFF[j]:OFF[j] + P], gw2_sb[:],
                                             start=True, stop=True)
                        last.then_inc(S["g2"], 1)
                    if name == "g4":
                        wait(pe, "c3", n + 1)
                        f = claim(1, "ct", n + 1)
                        transposes(f, c3, ROWS, OFF, KC).then_inc(S["g4"], 1)
                    if isinstance(name, int):
                        k, e = name, name // HC
                        if k == 0:
                            wait(pe, "ct", n + 1)
                            wait(pe, "xs", n + 1)
                            if n == 0:
                                pe.wait_ge(S["wsplit"], 2)
                                pe.wait_ge(S["init2"], 2)
                        if k % HC == 0:
                            wait(pe, "gs", NC * n + HC * (e - 1))
                            pe.matmul(CB[e % 2][:, 0:TE], sel[:, e, :], c_t[:, n, :], start=True, stop=True)\
                                .then_inc(S["cb"], 1)
                        wait(pe, "gl", NC * n + k - 1)
                        c = k % HC * 128
                        ph = PH[k % 2][:, 0:TE]
                        pe.matmul(ph, w1hi[:, e, c:c + 128], xhi[:, n, :], start=True, stop=False)
                        pe.matmul(ph, w1hi[:, e, c:c + 128], xlo[:, n, :], start=False, stop=False)
                        pe.matmul(ph, w1lo[:, e, c:c + 128], xhi[:, n, :], start=False, stop=True)\
                            .then_inc(S["l1"], 1)
                        if k == 1:
                            wait(pe, "yo", n)
                            pe.matmul(PY[:, 0:TE], be2hi[:], c_t[:, n, :], start=True, stop=False)
                        if k >= 2:
                            second_layer(n, k - 2)
                    if name == "flush":
                        second_layer(n, NC - 2)
                        second_layer(n, NC - 1)
                    if name == "out":
                        wait(pe, "yo", n + 1)
                        f = claim(2, "ob", n + 1)
                        for j in range(NJ):
                            last = pe.transpose(f[0:P, j * D:(j + 1) * D], yo[:, OFF[j]:OFF[j] + P], ident[:])
                        last.then_inc(S["ot"], 1)


_OUT = (B, TP, D)


def kernel(x, L0_tok_w_compress, L0_tok_b_compress, L0_tok_w_main, L0_tok_b_main, L0_tok_w_expand,
           L0_tok_b_expand, L0_tok_g_conv_norm, L0_tok_b_conv_norm, L0_tok_w_ff1, L0_tok_b_ff1, L0_tok_w_ff2,
           L0_tok_b_ff2, L0_tok_g_ff_norm, L0_tok_b_ff_norm, L0_attn_Wq, L0_attn_bq, L0_attn_Wk, L0_attn_bk,
           L0_ffn_gw1, L0_ffn_gb1, L0_ffn_gw2, L0_ffn_gb2, L0_ffn_we1, L0_ffn_be1, L0_ffn_we2, L0_ffn_be2):
    import numpy as np
    import concourse.bacc as bacc
    from concourse.bass_utils import run_bass_kernel_spmd

    def a(v, *order):
        v = np.asarray(v)
        return np.ascontiguousarray(v.transpose(order) if order else v)

    def col(v):
        return a(v).reshape(-1, 1)

    def row(v):
        return a(v).reshape(1, -1)

    host = {
        "x": a(x), "xt": a(x, 2, 0, 1),
        "wc": a(L0_tok_w_compress, 1, 2, 0).reshape(D, BN), "bc": col(L0_tok_b_compress),
        "wm": a(L0_tok_w_main, 1, 2, 0), "bm": col(L0_tok_b_main),
        "we": a(L0_tok_w_expand, 1, 2, 0).reshape(BN, D), "be": row(L0_tok_b_expand),
        "g1": row(L0_tok_g_conv_norm), "b1": row(L0_tok_b_conv_norm),
        "wf1": a(L0_tok_w_ff1, 1, 0), "bf1": col(L0_tok_b_ff1),
        "wf2": a(L0_tok_w_ff2, 1, 0), "bf2": row(L0_tok_b_ff2),
        "g2": row(L0_tok_g_ff_norm), "b2": row(L0_tok_b_ff_norm),
        "wq": a(L0_attn_Wq), "bq": col(L0_attn_bq), "wk": a(L0_attn_Wk), "bk": col(L0_attn_bk),
        "gw1": a(L0_ffn_gw1), "gb1": col(L0_ffn_gb1), "gw2": a(L0_ffn_gw2), "gb2": row(L0_ffn_gb2),
        "we1": a(L0_ffn_we1), "be1": a(np.asarray(L0_ffn_be1).reshape(NC, 128), 1, 0),
        "we2": a(L0_ffn_we2), "be2": a(L0_ffn_be2),
    }
    nc = bacc.Bacc("TRN2", target_bir_lowering=False, num_devices=1)
    aps = {k: nc.dram_tensor(f"in_{k}", v.shape, mybir.dt.from_np(v.dtype), kind="ExternalInput").ap()
           for k, v in host.items()}
    aps["out"] = nc.dram_tensor("out_0", _OUT, mybir.dt.float32, kind="ExternalOutput").ap()
    audio_tower(nc, **aps)
    r = run_bass_kernel_spmd(nc, [{f"in_{k}": v for k, v in host.items()}], core_ids=[0])
    return r.results[0]["out_0"]
```

```python
from contextlib import ExitStack

import concourse.bass as bass
from concourse import mybir

B, T, D = 8, 375, 128
BN = 64
TP = T - 2
E, H = 8, 256
NJ = 3
P = T // NJ
ROWS = [len(range(j, TP, NJ)) for j in range(NJ)]
OFF = [sum(ROWS[:j]) for j in range(NJ)]
TE = TP + 1
HC = H // 128
NC = E * HC
KC = 72
EPS = 1e-5
SCALE = float(D) ** -0.5

LAG = {"a1": 0, "a2": 0, "a3": 0, "a3b": 0,
       "a4": 1, "a5": 1, "a6": 1, "a6b": 1,
       "s3a": 2, "s3b": 2, "xnv": 2, "b1": 2, "b2": 2,
       "sc": 3, "pt": 3, "at": 3, "atb": 3,
       "h1": 4, "g1": 4, "g2": 4, "g3": 4, "g3b": 4, "g4": 4,
       "w1": 1, "w1lo": 2, "moe": 5, "yo": 6, "out": 6}
PE_ORDER = [0, 1, "a1", 2, "h1", 3, "a4", "a2", 4, "g1", 5, "a5", 6, 7, "a3", "g2", "a6", 8, 9, 10, "sc", 11, 12,
            "b1", "pt", 13, "b2", 14, 15, "at", "g4", "out", "flush"]
DVE_ORDER = [0, 1, "a1", 2, "s3a", 3, 4, "s3b", "a2", 5, 6, 7, "h1", "a3", "g2", 8, "a6", 9, "sc", 10, "a3b", "g3",
             "pt", 11, 12, "a6b", "b2", "g3b", 13, 14, 15, "at", "out", "atb"]
ACT_ORDER = ["yo", 0, 1, "a1", 2, 3, "h1", 4, "a4", 5, "a2", "g1", "a5", 6, 7, "w1", 8, "xnv", 9, 10, "g2", "sc", 11,
             "b1", 12, "pt", 13, "b2", "g3", 14, 15, "g4"]
PE_FILL = ["a1", "h1", "a4", "a2", "g1", "a5", "a3", "g2", "a6", "sc", "b1", "pt", "b2", "at", "g4", "out"]
DVE_FILL = ["a1", "s3a", "s3b", "a2", "h1", "a3", "g2", "a6", "sc", "a3b", "g3", "pt", "a6b", "b2", "g3b", "at",
            "out", "atb"]
ACT_FILL = ["yo", "a1", "h1", "a4", "a2", "g1", "a5", "w1", "xnv", "g2", "sc", "b1", "pt", "b2", "g3", "g4"]
POOL_ORDER = ["s3a", "a3", "a6", "a3b", "at", "w1lo"]
SP_ORDER = ["a6b", "out"]
STEPS = B + 6
LAG2 = 3
SC_BANK = [0, 1, 2]
PT_BANK = [1, 2, 0]


def pieces(order, t):
    for name in order:
        lag = LAG["moe" if name == "flush" or isinstance(name, int) else name]
        if 0 <= t - lag < B:
            yield name, t - lag


def audio_tower(nc, x, xt, wc, wm, we, wf1, wf2, wq, wk, gw1, gw2, b64, b128, b_rows, gb2, we1, we2, be2, out):
    fp32, fp32r, u32 = mybir.dt.float32, mybir.dt.float32r, mybir.dt.uint32
    ALU, ACT, AX = mybir.AluOpType, mybir.ActivationFunctionType, mybir.AxisListType

    with ExitStack() as ctx:
        def sb(name, shape, dt=fp32):
            return ctx.enter_context(nc.sbuf_tensor(name, shape, dt))

        def sem(name):
            return ctx.enter_context(nc.semaphore(name))

        x_sb = sb("x_sb", [P, B, NJ * D])
        xt_sb = sb("xt_sb", [D, B, T])
        wc_sb = sb("wc_sb", [D, BN])
        wm_sb = sb("wm_sb", [BN, 3, BN])
        we_sb = sb("we_sb", [BN, D])
        wf1_sb = sb("wf1_sb", [D, BN])
        wf2_sb = sb("wf2_sb", [BN, D])
        wq_sb = sb("wq_sb", [D, D])
        wk_sb = sb("wk_sb", [D, D])
        gw1_sb = sb("gw1_sb", [D, BN])
        gw2_sb = sb("gw2_sb", [BN, E])
        bias64 = sb("bias64", [BN, 8])
        bias128 = sb("bias128", [D, 2 + NC])
        rows = sb("rows", [P, 6 * D])
        gb2_sb = sb("gb2_sb", [P, NJ * E])
        w1_sb = sb("w1_sb", [D, E, H])
        w1hi = sb("w1hi", [D, E, H], fp32r)
        w1lo = sb("w1lo", [D, E, H], fp32r)
        w2_sb = sb("w2_sb", [128, NC, D])
        be2_sb = sb("be2_sb", [KC, D])
        be2hi = sb("be2hi", [KC, D], fp32r)
        ident = sb("ident", [128, 128])
        sel32 = sb("sel32", [KC, E, D])
        sel = sb("sel", [KC, E, D], fp32r)
        iota_e = sb("iota_e", [P, NJ, E])
        mhalf = sb("mhalf", [P, NJ])

        th1, z1 = sb("th1", [BN, T]), sb("z1", [BN, T])
        th2, z2 = sb("th2", [BN, T]), sb("z2", [BN, T])
        hc1 = sb("hc1", [BN, T + 2])
        hc2 = sb("hc2", [BN, T])
        r1 = sb("r1", [P, NJ, D])
        n1 = sb("n1", [P, NJ, D])
        y = sb("y", [P, NJ, D])
        yb = sb("yb", [P, NJ, D])
        y_t = sb("y_t", [D, T])
        f1 = sb("f1", [BN, T])
        r2 = sb("r2", [P, NJ, D])
        n2 = sb("n2", [P, NJ, D])
        y2 = sb("y2", [P, NJ, D])
        y2next = sb("y2next", [P, 2, D])
        m12 = sb("m12", [P, D])
        m01 = sb("m01", [P, D])
        h = sb("h", [P, B, NJ * D])
        xn3 = sb("xn3", [P, NJ, D])
        xn3v = sb("xn3v", [P, B, NJ * D])
        xn_t = sb("xn_t", [D, TP])
        q_t = sb("q_t", [D, TE])
        k_t = sb("k_t", [D, TP])
        nmax = sb("nmax", [P, NJ])
        prob = sb("prob", [P, NJ, TP])
        psum_row = sb("psum_row", [P, NJ])
        rinv = sb("rinv", [P, NJ])
        prob_t = sb("prob_t", [P, NJ, TE])
        h2 = sb("h2", [P, B, NJ * D])
        xn4 = sb("xn4", [P, NJ, D])
        x32 = sb("x32", [D, TP])
        xhi = sb("xhi", [D, B, TE], fp32r)
        xlo = sb("xlo", [D, B, TE], fp32r)
        gh_t = sb("gh_t", [BN, TE])
        lg = sb("lg", [P, NJ, E])
        lmax = sb("lmax", [P, NJ])
        le = sb("le", [P, NJ, E])
        ge = sb("ge", [P, NJ, E])
        gsum = sb("gsum", [P, NJ])
        grec = sb("grec", [P, NJ])
        gp = sb("gp", [P, NJ, E])
        top = sb("top", [P, NJ, 8])
        topi = sb("topi", [P, NJ, 8], u32)
        topf = sb("topf", [P, NJ, 2])
        dd = sb("dd", [P, NJ])
        th3 = sb("th3", [P, NJ])
        w_top = sb("w_top", [P, 2, NJ])
        one1, one2 = sb("one1", [P, NJ, E]), sb("one2", [P, NJ, E])
        s1, s2 = sb("s1", [P, NJ, E]), sb("s2", [P, NJ, E])
        comb = sb("comb", [P, NJ, E])
        chi = sb("chi", [P, NJ, E], fp32r)
        c3 = sb("c3", [P, NJ, KC])
        c_t = sb("c_t", [KC, B, TE], fp32r)
        g_sb = [sb(f"g_sb{i}", [128, TP]) for i in range(4)]
        gs_sb = [sb(f"gs_sb{i}", [128, TP]) for i in range(4)]
        yo = sb("yo", [D, TE])
        ob = sb("ob", [P, NJ * D])
        stat = [sb(f"stat{i}", [P, NJ, 6]) for i in range(4)]
        mv = [sb(f"mv{i}", [P, NJ, 2]) for i in range(4)]
        ve = [sb(f"ve{i}", [P, NJ]) for i in range(4)]
        rstd = [sb(f"rstd{i}", [P, NJ]) for i in range(4)]

        def bank(name):
            return ctx.enter_context(nc.psum_tensor(name, [128, 512], fp32))

        F = [bank(f"F{i}") for i in range(3)]
        PH = [bank(f"PH{i}") for i in range(2)]
        CB = [bank(f"CB{i}") for i in range(2)]
        PY = bank("PY")

        names = """rows wearly wmid wlate xb ident init init2 wsplit
            h1 x32 xs g1 gh g2 le ge g3 dd th3 c3 g4 ct
            a1 z1 hc1 a2 z2 hc2 a3 y yb a4 yt a5 f1 a6 y2 shift xn3 xnv b1 xnt qp kp q k
            sc nmax prob pt pta ptd at xn4 cb l1 gl gs l2 yo ot ob out r1 r2 h2 lg be2 one dve act""".split()
        S = {n: sem("s_" + n) for n in names}
        s_x = [sem(f"s_x{b}") for b in range(B)]
        s_xt = [sem(f"s_xt{b}") for b in range(B)]
        s_ve = [sem(f"s_ve{i}") for i in range(4)]
        s_rstd = [sem(f"s_rstd{i}") for i in range(4)]

        def wait(eng, name, value):
            if value > 0:
                eng.wait_ge(S[name], value)

        block = ctx.enter_context(nc.Block())

        @block.sync
        def _(sp):
            sp.dma_start(wc_sb[:], wc).then_inc(S["wearly"], 16)
            sp.dma_start(wm_sb[:], wm).then_inc(S["wearly"], 16)
            sp.dma_start(we_sb[:], we).then_inc(S["wearly"], 16)
            for b in range(B):
                sp.dma_start(xt_sb[:, b, :], xt[:, b, :]).then_inc(s_xt[b], 16)
                sp.dma_start(x_sb[:, b, :], x[b].rearrange("(p j) d -> p (j d)", j=NJ)).then_inc(s_x[b], 16)
                if b == 0:
                    sp.dma_start(rows[:], b_rows.broadcast_to([P, 6 * D])).then_inc(S["rows"], 16)
                    for dst, src in ((wf1_sb, wf1), (wf2_sb, wf2), (bias128, b128), (wq_sb, wq), (wk_sb, wk),
                                     (gw1_sb, gw1), (gw2_sb, gw2)):
                        sp.dma_start(dst[:], src).then_inc(S["wmid"], 16)
                    sp.dma_start(gb2_sb[:], gb2.broadcast_to([P, NJ * E])).then_inc(S["wmid"], 16)
            sp.dma_start(w1_sb[:], we1.rearrange("e d h -> d e h")).then_inc(S["wlate"], 16)
            sp.dma_start(w2_sb[:], we2.rearrange("e (c p) d -> p (e c) d", p=128)).then_inc(S["wlate"], 16)
            for t in range(STEPS + 1):
                for name, n in pieces(SP_ORDER, t):
                    if name == "a6b":
                        wait(sp, "y2", n + 1)
                        sp.dma_start(y2next[0:P - 1, :, :], y2[1:P, 0:2, :]).then_inc(S["shift"], 16)
                    if name == "out":
                        wait(sp, "ob", n + 1)
                        sp.dma_start(out[n, 0:TP - 1, :].rearrange("(p j) d -> p (j d)", j=NJ),
                                     ob[0:P - 1, :]).then_inc(S["out"], 16)
                        sp.dma_start(out[n, TP - 1:TP, :], ob[P - 1:P, 0:D]).then_inc(S["out"], 16)
            sp.wait_ge(S["out"], 32 * B)

        def pool_piece(pool, name, n):
            ln = {"a3": 0, "a6": 1, "s3a": 2, "at": 3}.get(name)
            if ln is not None:
                pool.wait_ge(s_ve[ln], n + 1)
                pool.tensor_tensor(rstd[ln][:], ve[ln][:], mhalf[:], ALU.pow).then_inc(s_rstd[ln], 1)
            if name == "w1lo" and n == 0:
                pool.wait_ge(S["wsplit"], 1)
                pool.tensor_tensor(w1lo[:], w1_sb[:], w1hi[:].bitcast(fp32), ALU.subtract).then_inc(S["wsplit"], 1)
            if name == "a3b":
                wait(pool, "y", n + 1)
                pool.tensor_tensor(yb[:], y[:], rows[:, 3 * D:4 * D].unsqueeze(1).broadcast_to([P, NJ, D]), ALU.add)\
                    .then_inc(S["yb"], 1)

        @block.gpsimd
        def _(pool):
            pool.memset(ident[:], 0.0).then_inc(S["ident"], 1)
            pool.memset(sel32[:], 0.0).then_inc(S["ident"], 1)
            pool.wait_ge(S["ident"], 2)
            pool.affine_select(out=ident[:], in_=ident[:], compare_op=ALU.not_equal, fill=1.0, base=0,
                               pattern=[[-1, 128]], channel_multiplier=1).then_inc(S["ident"], 1)
            for i, r in enumerate((0, 32)):
                pool.wait_ge(S["ident"], 3 + i)
                v = sel32[r:r + E, :, :]
                pool.affine_select(out=v, in_=v, compare_op=ALU.not_equal, fill=1.0, base=0,
                                   pattern=[[-1, E], [0, D]], channel_multiplier=1).then_inc(S["ident"], 1)
            pool.wait_ge(S["ident"], 5)
            pool.iota(iota_e[:], [[0, NJ], [1, E]], base=0, channel_multiplier=0,
                      allow_small_or_imprecise_dtypes=True).then_inc(S["init"], 1)
            pool.memset(mhalf[:], -0.5).then_inc(S["init"], 1)
            for v in (hc1[:, 0:1], hc1[:, T + 1:T + 2], q_t[:, TP:TE], prob_t[:, :, TP:TE], gh_t[:, TP:TE],
                      yo[:, TP:TE], y2next[:], c3[:], be2_sb[:]):
                pool.memset(v, 0.0).then_inc(S["init"], 1)
            for v in (xhi[:, :, TP:TE], xlo[:, :, TP:TE], c_t[:, :, TP:TE]):
                pool.memset(v.bitcast(fp32), 0.0).then_inc(S["init"], 1)
            pool.wait_ge(S["rows"], 16)
            for b in range(B):
                pool.wait_ge(s_x[b], 16)
                v = x_sb[:, b, :].rearrange("p (j d) -> p j d", j=NJ)
                pool.tensor_tensor(v, v, rows[:, 0:D].unsqueeze(1).broadcast_to([P, NJ, D]), ALU.add).then_inc(S["xb"], 1)
                if b == 0:
                    first = list(pieces(POOL_ORDER, 0))
                    for name, n in first:
                        pool_piece(pool, name, n)
            for t in range(1, STEPS + 1):
                for name, n in pieces(POOL_ORDER, t):
                    pool_piece(pool, name, n)

        @block.scalar
        def _(act):
            act.dma_start(bias64[:, 0:4], b64).then_inc(S["wearly"], 16)
            act.wait_ge(S["wearly"], 16 * 4)
            act.activation(bias64[:, 4:6], bias64[:, 0:2], ACT.Copy, scale=0.5).then_inc(S["act"], 1)
            act.wait_ge(S["act"], 1)

            for t in range(STEPS + 1):
                for name, n in pieces(ACT_ORDER if t >= LAG["moe"] else ACT_FILL, t):
                    if name == "a1":
                        wait(act, "a1", n + 1)
                        wait(act, "hc1", n)
                        act.activation(th1[:], F[2][0:BN, 0:T], ACT.Tanh, bias=bias64[:, 4:5], scale=0.5)
                        act.activation(z1[:], F[2][0:BN, 0:T], ACT.Identity, bias=bias64[:, 4:5], scale=0.5)\
                            .then_inc(S["z1"], 1)
                    if name == "a2":
                        wait(act, "a2", n + 1)
                        wait(act, "hc2", n)
                        act.activation(th2[:], F[0][0:BN, 0:T], ACT.Tanh, bias=bias64[:, 5:6], scale=0.5)
                        act.activation(z2[:], F[0][0:BN, 0:T], ACT.Identity, bias=bias64[:, 5:6], scale=0.5)\
                            .then_inc(S["z2"], 1)
                    if name == "a4":
                        wait(act, "a4", n + 1)
                        if n == 0:
                            act.wait_ge(S["wmid"], 16 * 8)
                        act.activation(y_t[:], F[2][:, 0:T], ACT.Copy).then_inc(S["yt"], 1)
                    if name == "a5":
                        wait(act, "a5", n + 1)
                        act.activation(f1[:], F[2][0:BN, 0:T], ACT.Gelu, bias=bias64[:, 2:3]).then_inc(S["f1"], 1)
                    if name == "w1" and n == 0:
                        act.wait_ge(S["init"], 14)
                        for r in (0, 32, 64):
                            act.dma_start(be2_sb[r:r + E, :], be2).then_inc(S["be2"], 16)
                        act.wait_ge(S["wlate"], 16 * 2)
                        act.activation(w1hi[:], w1_sb[:], ACT.Copy).then_inc(S["wsplit"], 1)
                    if name == "xnv":
                        wait(act, "xn3", n + 1)
                        act.activation(xn3v[:, n, :], xn3[:].rearrange("p j d -> p (j d)"), ACT.Copy)\
                            .then_inc(S["xnv"], 1)
                    if name == "b1":
                        wait(act, "b1", n + 1)
                        act.activation(xn_t[:], F[0][:, 0:TP], ACT.Copy).then_inc(S["xnt"], 1)
                    if name == "b2":
                        wait(act, "kp", n + 1)
                        act.activation(k_t[:], F[2][:, 0:TP], ACT.Identity, bias=bias128[:, 1:2])\
                            .then_inc(S["k"], 1)
                    if name == "sc":
                        for j in range(NJ):
                            wait(act, "nmax", NJ * n + j + 1)
                            act.activation(prob[:, j, :], F[SC_BANK[j]][0:P, 0:TP], ACT.Exp, bias=nmax[:, j:j + 1],
                                           accum_out=psum_row[:, j:j + 1]).then_inc(S["prob"], 1)
                    if name == "g2":
                        wait(act, "le", n + 1)
                        act.activation(ge[:], le[:], ACT.Exp).then_inc(S["ge"], 1)
                    if name == "pt":
                        for c in (0, 2):
                            wait(act, "pt", NJ * n + c + 1)
                            act.activation(prob_t[0:ROWS[c], c, 0:TP], F[PT_BANK[c]][0:ROWS[c], 0:TP], ACT.Copy)\
                                .then_inc(S["pta"], 1)
                    if name == "h1":
                        wait(act, "h1", n + 1)
                        wait(act, "xs", n)
                        act.activation(x32[:], F[1][:, 0:TP], ACT.Copy).then_inc(S["x32"], 1)
                    if name == "g1":
                        wait(act, "g1", n + 1)
                        act.activation(gh_t[:, 0:TP], F[1][0:BN, 0:TP], ACT.Relu, bias=bias64[:, 3:4])\
                            .then_inc(S["gh"], 1)
                    if name == "g3":
                        wait(act, "dd", n + 1)
                        act.activation(th3[:], dd[:], ACT.Tanh, scale=0.5).then_inc(S["th3"], 1)
                    if name == "g4":
                        wait(act, "g4", n + 1)
                        act.activation(c_t[:, n, 0:TP], F[2][0:KC, 0:TP], ACT.Copy).then_inc(S["ct"], 1)
                    if isinstance(name, int):
                        k = name
                        wait(act, "l1", NC * n + k + 1)
                        wait(act, "gs", NC * n + k - 3)
                        act.activation(g_sb[k % 4][:], PH[k % 2][:, 0:TP], ACT.Gelu, bias=bias128[:, 2 + k:3 + k])\
                            .then_inc(S["gl"], 1)
                    if name == "yo":
                        wait(act, "l2", NC * (n + 1))
                        wait(act, "ot", n)
                        act.activation(yo[:, 0:TP], PY[:, 0:TP], ACT.Copy).then_inc(S["yo"], 1)

        @block.vector
        def _(dve):
            chain = [0]

            def link(ins):
                chain[0] += 1
                ins.then_inc(S["dve"], 1)
                dve.wait_ge(S["dve"], chain[0])

            def bc(ap):
                return ap.broadcast_to([P, NJ, E])

            def ln_stats(i, src):
                for j in range(NJ):
                    last = dve.bn_stats(stat[i][:, j, :], src[j])
                link(last)
                for j in range(NJ):
                    last = dve.bn_aggr(mv[i][:, j, :], stat[i][:, j, :])
                link(last)
                dve.tensor_scalar(ve[i][:], mv[i][:, :, 1], EPS, None, ALU.add).then_inc(s_ve[i], 1)

            def ln_apply(i, n, src, dst):
                dve.wait_ge(s_rstd[i], n + 1)
                for j in range(NJ):
                    last = dve.tensor_scalar(dst[j], src[j], mv[i][:, j, 0:1], rstd[i][:, j:j + 1],
                                             ALU.subtract, ALU.mult)
                return last

            def tiles(ap):
                return [ap[:, j, :] for j in range(NJ)]

            def flat_tiles(ap, n):
                return [ap[:, n, j * D:(j + 1) * D] for j in range(NJ)]

            def row(i):
                return rows[:, i * D:(i + 1) * D].unsqueeze(1).broadcast_to([P, NJ, D])

            dve.wait_ge(S["ident"], 5)
            dve.tensor_copy(sel[:], sel32[:]).then_inc(S["init2"], 1)
            for t in range(STEPS + 1):
                for name, n in pieces(DVE_ORDER if t >= LAG["moe"] else DVE_FILL, t):
                    if name == "a1":
                        wait(dve, "z1", n + 1)
                        if n == 0:
                            dve.wait_ge(S["init"], 14)
                        dve.scalar_tensor_tensor(hc1[:, 1:T + 1], th1[:], 1.0, z1[:], ALU.add, ALU.mult)\
                            .then_inc(S["hc1"], 1)
                    if name == "a2":
                        wait(dve, "z2", n + 1)
                        dve.scalar_tensor_tensor(hc2[:], th2[:], 1.0, z2[:], ALU.add, ALU.mult)\
                            .then_inc(S["hc2"], 1)
                    if name == "a3":
                        wait(dve, "a3", n + 1)
                        wait(dve, "xb", n + 1)
                        dve.tensor_tensor(r1[:].rearrange("p j d -> p (j d)"), F[0][0:P, 0:NJ * D],
                                          x_sb[:, n, :], ALU.add).then_inc(S["r1"], 1)
                        wait(dve, "r1", n + 1)
                        ln_stats(0, tiles(r1))
                    if name == "a3b":
                        link(ln_apply(0, n, tiles(r1), tiles(n1)))
                        link(dve.tensor_tensor(n1[:], n1[:], row(1), ALU.mult))
                        wait(dve, "a4", n)
                        wait(dve, "yb", n)
                        dve.tensor_tensor(y[:], n1[:], row(2), ALU.add).then_inc(S["y"], 1)
                    if name == "a6":
                        wait(dve, "a6", n + 1)
                        wait(dve, "yb", n + 1)
                        dve.tensor_tensor(r2[:].rearrange("p j d -> p (j d)"), F[2][0:P, 0:NJ * D],
                                          yb[:].rearrange("p j d -> p (j d)"), ALU.add).then_inc(S["r2"], 1)
                        wait(dve, "r2", n + 1)
                        ln_stats(1, tiles(r2))
                    if name == "a6b":
                        link(ln_apply(1, n, tiles(r2), tiles(n2)))
                        link(dve.tensor_tensor(n2[:], n2[:], row(4), ALU.mult))
                        dve.tensor_tensor(y2[:], n2[:], row(5), ALU.add).then_inc(S["y2"], 1)
                    if name == "s3a" and n == 0:
                        dve.wait_ge(S["be2"], 16 * 3)
                        link(dve.tensor_copy(be2hi[:], be2_sb[:]))
                        link(dve.tensor_tensor(be2_sb[64:KC, :], be2_sb[64:KC, :], be2hi[64:KC, :].bitcast(fp32), ALU.subtract))
                        dve.tensor_copy(be2hi[64:KC, :], be2_sb[64:KC, :]).then_inc(S["init2"], 1)
                    if name == "s3a":
                        wait(dve, "y2", n + 1)
                        wait(dve, "shift", 16 * (n + 1))
                        hn = flat_tiles(h, n)
                        dve.tensor_tensor(m12[:], y2[:, 1, :], y2[:, 2, :], ALU.max)
                        link(dve.tensor_tensor(m01[:], y2next[:, 0, :], y2next[:, 1, :], ALU.max))
                        dve.tensor_tensor(hn[0], y2[:, 0, :], m12[:], ALU.max)
                        dve.tensor_tensor(hn[1], m12[:], y2next[:, 0, :], ALU.max)
                        link(dve.tensor_tensor(hn[2], y2[:, 2, :], m01[:], ALU.max))
                        ln_stats(2, hn)
                    if name == "s3b":
                        wait(dve, "b1", n)
                        wait(dve, "xnv", n)
                        ln_apply(2, n, flat_tiles(h, n), tiles(xn3)).then_inc(S["xn3"], 1)
                    if name == "b2":
                        wait(dve, "qp", n + 1)
                        dve.tensor_scalar(q_t[:, 0:TP], F[1][:, 0:TP], bias128[:, 0:1], SCALE, ALU.add, ALU.mult)\
                            .then_inc(S["q"], 1)
                    if name == "sc":
                        for j in range(NJ):
                            wait(dve, "sc", NJ * n + j + 1)
                            dve.tensor_reduce(nmax[:, j:j + 1], F[SC_BANK[j]][0:P, 0:TP], AX.X, ALU.max, negate=True)\
                                .then_inc(S["nmax"], 1)
                    if name == "pt":
                        wait(dve, "pt", NJ * n + 2)
                        dve.tensor_copy(prob_t[0:ROWS[1], 1, 0:TP], F[PT_BANK[1]][0:ROWS[1], 0:TP]).then_inc(S["ptd"], 1)
                    if name == "at":
                        wait(dve, "prob", NJ * (n + 1))
                        link(dve.reciprocal(rinv[:], psum_row[:]))
                        wait(dve, "at", n + 1)
                        for j in range(NJ):
                            last = dve.scalar_tensor_tensor(flat_tiles(h2, n)[j], F[0][0:P, j * D:(j + 1) * D],
                                                            rinv[:, j:j + 1], flat_tiles(h, n)[j], ALU.mult, ALU.add)
                        last.then_inc(S["h2"], 1)
                        wait(dve, "h2", n + 1)
                        ln_stats(3, flat_tiles(h2, n))
                    if name == "atb":
                        wait(dve, "h1", n)
                        ln_apply(3, n, flat_tiles(h2, n), tiles(xn4)).then_inc(S["xn4"], 1)
                    if name == "h1":
                        wait(dve, "x32", n + 1)
                        link(dve.tensor_copy(xhi[:, n, 0:TP], x32[:]))
                        dve.tensor_tensor(xlo[:, n, 0:TP], x32[:], xhi[:, n, 0:TP].bitcast(fp32), ALU.subtract)\
                            .then_inc(S["xs"], 1)
                    if name == "g2":
                        wait(dve, "g2", n + 1)
                        dve.tensor_tensor(lg[:], F[1][0:P, 0:NJ * E].rearrange("p (j e) -> p j e", j=NJ),
                                          gb2_sb[:].rearrange("p (j e) -> p j e", j=NJ), ALU.add).then_inc(S["lg"], 1)
                        wait(dve, "lg", n + 1)
                        link(dve.tensor_reduce(lmax[:], lg[:], AX.X, ALU.max))
                        dve.tensor_tensor(le[:], lg[:], bc(lmax[:].unsqueeze(2)), ALU.subtract).then_inc(S["le"], 1)
                    if name == "g3":
                        wait(dve, "ge", n + 1)
                        link(dve.tensor_reduce(gsum[:], ge[:], AX.X, ALU.add))
                        link(dve.reciprocal(grec[:], gsum[:]))
                        link(dve.tensor_tensor(gp[:], ge[:], bc(grec[:].unsqueeze(2)), ALU.mult))
                        for j in range(NJ):
                            last = dve.max(top[:, j, :], gp[:, j, :])
                        link(last)
                        dve.tensor_tensor(dd[:], top[:, :, 1], top[:, :, 0], ALU.subtract).then_inc(S["dd"], 1)
                        for j in range(NJ):
                            last = dve.max_index(topi[:, j, :], top[:, j, :], gp[:, j, :])
                        link(last)
                        link(dve.tensor_copy(topf[:], topi[:, :, 0:2]))
                        dve.tensor_tensor(one1[:], iota_e[:], bc(topf[:, :, 0:1]), ALU.is_equal)
                        last = dve.tensor_tensor(one2[:], iota_e[:], bc(topf[:, :, 1:2]), ALU.is_equal)
                        last.then_inc(S["one"], 1)
                    if name == "g3b":
                        wait(dve, "th3", n + 1)
                        wait(dve, "one", n + 1)
                        dve.tensor_scalar(w_top[:, 0, :], th3[:], -0.5, 0.5, ALU.mult, ALU.add)
                        link(dve.tensor_scalar(w_top[:, 1, :], th3[:], 0.5, 0.5, ALU.mult, ALU.add))
                        dve.tensor_tensor(s1[:], one1[:], bc(w_top[:, 0, :].unsqueeze(2)), ALU.mult)
                        link(dve.tensor_tensor(s2[:], one2[:], bc(w_top[:, 1, :].unsqueeze(2)), ALU.mult))
                        link(dve.tensor_tensor(comb[:], s1[:], s2[:], ALU.add))
                        link(dve.tensor_copy(chi[:], comb[:]))
                        wait(dve, "g4", n)
                        dve.tensor_copy(c3[:, :, 0:E], chi[:].bitcast(fp32))
                        dve.tensor_copy(c3[:, :, 64:64 + E], chi[:].bitcast(fp32))
                        dve.tensor_tensor(c3[:, :, 32:32 + E], comb[:], chi[:].bitcast(fp32), ALU.subtract)\
                            .then_inc(S["c3"], 1)
                    if isinstance(name, int):
                        k = name
                        wait(dve, "gl", NC * n + k + 1)
                        wait(dve, "cb", E * n + k // HC + 1)
                        wait(dve, "l2", NC * n + k - 3)
                        dve.tensor_tensor(gs_sb[k % 4][:], g_sb[k % 4][:], CB[k // HC % 2][:, 0:TP], ALU.mult)\
                            .then_inc(S["gs"], 1)
                    if name == "out":
                        wait(dve, "ot", n + 1)
                        wait(dve, "out", 32 * n)
                        dve.tensor_tensor(ob[:], F[1][0:P, 0:NJ * D], h2[:, n, :], ALU.add).then_inc(S["ob"], 1)

        @block.tensor
        def _(pe):
            reader = [None] * 3

            def claim(f, name, value):
                if reader[f]:
                    wait(pe, *reader[f])
                reader[f] = (name, value)
                return F[f]

            def transposes(dst, src, rows_of, off, width=D):
                for j in range(NJ):
                    last = pe.transpose(dst[0:width, off[j]:off[j] + rows_of[j]], src[0:rows_of[j], j, 0:width],
                                        ident[0:rows_of[j], 0:rows_of[j]])
                return last

            def second_layer(n, k):
                wait(pe, "gs", NC * n + k + 1)
                pe.matmul(PY[:, 0:TP], w2_sb[:, k, :], gs_sb[k % 4][:], start=False, stop=(k == NC - 1))\
                    .then_inc(S["l2"], 1)

            pe.wait_ge(S["ident"], 5)
            pe.wait_ge(S["wearly"], 16 * 4)
            for t in range(STEPS + 1):
                for name, n in pieces(PE_ORDER if t >= LAG["moe"] else PE_FILL, t):
                    if name == "a1":
                        pe.wait_ge(s_xt[n], 16)
                        f = claim(2, "z1", n + 1)
                        pe.matmul(f[0:BN, 0:T], wc_sb[:], xt_sb[:, n, :], start=True, stop=True).then_inc(S["a1"], 1)
                    if name == "a2":
                        wait(pe, "hc1", n + 1)
                        f = claim(0, "z2", n + 1)
                        for k in range(3):
                            last = pe.matmul(f[0:BN, 0:T], wm_sb[:, k, :], hc1[:, k:k + T],
                                             start=(k == 0), stop=(k == 2))
                        last.then_inc(S["a2"], 1)
                    if name == "a3":
                        wait(pe, "hc2", n + 1)
                        f = claim(0, "r1", n + 1)
                        for j in range(NJ):
                            last = pe.matmul(f[0:P, j * D:(j + 1) * D], hc2[:, j:T:NJ], we_sb[:],
                                             start=True, stop=True)
                        last.then_inc(S["a3"], 1)
                    if name == "a4":
                        wait(pe, "y", n + 1)
                        f = claim(2, "yt", n + 1)
                        transposes(f, y, [P] * NJ, [P * j for j in range(NJ)]).then_inc(S["a4"], 1)
                    if name == "a5":
                        wait(pe, "yt", n + 1)
                        if n == 0:
                            pe.wait_ge(S["wmid"], 16 * 8)
                        f = claim(2, "f1", n + 1)
                        pe.matmul(f[0:BN, 0:T], wf1_sb[:], y_t[:], start=True, stop=True).then_inc(S["a5"], 1)
                    if name == "a6":
                        wait(pe, "f1", n + 1)
                        f = claim(2, "r2", n + 1)
                        for j in range(NJ):
                            last = pe.matmul(f[0:P, j * D:(j + 1) * D], f1[:, j * P:(j + 1) * P], wf2_sb[:],
                                             start=True, stop=True)
                        last.then_inc(S["a6"], 1)
                    if name == "b1":
                        wait(pe, "xn3", n + 1)
                        f = claim(0, "xnt", n + 1)
                        transposes(f, xn3, ROWS, OFF).then_inc(S["b1"], 1)
                    if name == "b2":
                        wait(pe, "xnt", n + 1)
                        f = claim(1, "q", n + 1)
                        pe.matmul(f[:, 0:TP], wq_sb[:], xn_t[:], start=True, stop=True).then_inc(S["qp"], 1)
                        f = claim(2, "k", n + 1)
                        pe.matmul(f[:, 0:TP], wk_sb[:], xn_t[:], start=True, stop=True).then_inc(S["kp"], 1)
                    if name == "sc":
                        wait(pe, "q", n + 1)
                        wait(pe, "k", n + 1)
                        for j in range(NJ):
                            f = claim(SC_BANK[j], "prob", NJ * n + j + 1)
                            pe.matmul(f[0:P, 0:TP], q_t[:, OFF[j]:OFF[j] + P], k_t[:], start=True, stop=True)\
                                .then_inc(S["sc"], 1)
                    if name == "pt":
                        wait(pe, "prob", NJ * (n + 1))
                        for c in range(NJ):
                            f = claim(PT_BANK[c], *(("ptd", n + 1) if c == 1 else ("pta", 2 * n + c // 2 + 1)))
                            for j in range(NJ):
                                last = pe.transpose(f[0:ROWS[c], OFF[j]:OFF[j] + ROWS[j]],
                                                    prob[0:ROWS[j], j, OFF[c]:OFF[c] + ROWS[c]],
                                                    ident[0:ROWS[j], 0:ROWS[j]])
                            last.then_inc(S["pt"], 1)
                    if name == "at":
                        wait(pe, "pta", 2 * (n + 1))
                        wait(pe, "ptd", n + 1)
                        wait(pe, "xnv", n + 1)
                        f = claim(0, "h2", n + 1)
                        for j in range(NJ):
                            for c in range(NJ):
                                last = pe.matmul(f[0:P, j * D:(j + 1) * D],
                                                 prob_t[0:ROWS[c], c, OFF[j]:OFF[j] + P],
                                                 xn3v[0:ROWS[c], n, c * D:(c + 1) * D],
                                                 start=(c == 0), stop=(c == NJ - 1))
                        last.then_inc(S["at"], 1)
                    if name == "h1":
                        wait(pe, "xn4", n + 1)
                        f = claim(1, "x32", n + 1)
                        transposes(f, xn4, ROWS, OFF).then_inc(S["h1"], 1)
                    if name == "g1":
                        wait(pe, "x32", n + 1)
                        f = claim(1, "gh", n + 1)
                        pe.matmul(f[0:BN, 0:TP], gw1_sb[:], x32[:], start=True, stop=True).then_inc(S["g1"], 1)
                    if name == "g2":
                        wait(pe, "gh", n + 1)
                        f = claim(1, "lg", n + 1)
                        for j in range(NJ):
                            last = pe.matmul(f[0:P, j * E:(j + 1) * E], gh_t[:, OFF[j]:OFF[j] + P], gw2_sb[:],
                                             start=True, stop=True)
                        last.then_inc(S["g2"], 1)
                    if name == "g4":
                        wait(pe, "c3", n + 1)
                        f = claim(2, "ct", n + 1)
                        transposes(f, c3, ROWS, OFF, KC).then_inc(S["g4"], 1)
                    if isinstance(name, int):
                        k, e = name, name // HC
                        if k == 0:
                            wait(pe, "ct", n + 1)
                            wait(pe, "xs", n + 1)
                            if n == 0:
                                pe.wait_ge(S["wsplit"], 2)
                                pe.wait_ge(S["init2"], 2)
                        if k % HC == 0:
                            wait(pe, "gs", NC * n + HC * (e - 1))
                            pe.matmul(CB[e % 2][:, 0:TE], sel[:, e, :], c_t[:, n, :], start=True, stop=True)\
                                .then_inc(S["cb"], 1)
                        wait(pe, "gl", NC * n + k - 1)
                        c = k % HC * 128
                        ph = PH[k % 2][:, 0:TE]
                        pe.matmul(ph, w1hi[:, e, c:c + 128], xhi[:, n, :], start=True, stop=False)
                        pe.matmul(ph, w1hi[:, e, c:c + 128], xlo[:, n, :], start=False, stop=False)
                        pe.matmul(ph, w1lo[:, e, c:c + 128], xhi[:, n, :], start=False, stop=True)\
                            .then_inc(S["l1"], 1)
                        if k == 2:
                            wait(pe, "yo", n)
                            pe.matmul(PY[:, 0:TE], be2hi[:], c_t[:, n, :], start=True, stop=False)
                        if k >= LAG2:
                            second_layer(n, k - LAG2)
                    if name == "flush":
                        for k in range(NC - LAG2, NC):
                            second_layer(n, k)
                    if name == "out":
                        wait(pe, "yo", n + 1)
                        f = claim(1, "ob", n + 1)
                        for j in range(NJ):
                            last = pe.transpose(f[0:P, j * D:(j + 1) * D], yo[:, OFF[j]:OFF[j] + P], ident[:])
                        last.then_inc(S["ot"], 1)


_OUT = (B, TP, D)


def kernel(x, L0_tok_w_compress, L0_tok_b_compress, L0_tok_w_main, L0_tok_b_main, L0_tok_w_expand,
           L0_tok_b_expand, L0_tok_g_conv_norm, L0_tok_b_conv_norm, L0_tok_w_ff1, L0_tok_b_ff1, L0_tok_w_ff2,
           L0_tok_b_ff2, L0_tok_g_ff_norm, L0_tok_b_ff_norm, L0_attn_Wq, L0_attn_bq, L0_attn_Wk, L0_attn_bk,
           L0_ffn_gw1, L0_ffn_gb1, L0_ffn_gw2, L0_ffn_gb2, L0_ffn_we1, L0_ffn_be1, L0_ffn_we2, L0_ffn_be2):
    import numpy as np
    import concourse.bacc as bacc
    from concourse.bass_utils import run_bass_kernel_spmd

    def a(v, *order):
        v = np.asarray(v)
        return np.ascontiguousarray(v.transpose(order) if order else v)

    def cols(*vs):
        return np.ascontiguousarray(np.stack([np.asarray(v) for v in vs], axis=1))

    host = {
        "x": a(x), "xt": a(x, 2, 0, 1),
        "wc": a(L0_tok_w_compress, 1, 2, 0).reshape(D, BN), "wm": a(L0_tok_w_main, 1, 2, 0),
        "we": a(L0_tok_w_expand, 1, 2, 0).reshape(BN, D),
        "wf1": a(L0_tok_w_ff1, 1, 0), "wf2": a(L0_tok_w_ff2, 1, 0),
        "wq": a(L0_attn_Wq), "wk": a(L0_attn_Wk), "gw1": a(L0_ffn_gw1), "gw2": a(L0_ffn_gw2),
        "we1": a(L0_ffn_we1), "we2": a(L0_ffn_we2), "be2": a(L0_ffn_be2),
        "b64": cols(L0_tok_b_compress, L0_tok_b_main, L0_tok_b_ff1, L0_ffn_gb1),
        "b128": cols(L0_attn_bq, L0_attn_bk, *np.asarray(L0_ffn_be1).reshape(NC, 128)),
        "b_rows": np.concatenate([np.asarray(v) for v in (
            L0_tok_b_expand, L0_tok_g_conv_norm, L0_tok_b_conv_norm, L0_tok_b_ff2, L0_tok_g_ff_norm,
            L0_tok_b_ff_norm)]).reshape(1, 6 * D),
        "gb2": np.concatenate([np.asarray(L0_ffn_gb2)] * NJ).reshape(1, NJ * E),
    }
    nc = bacc.Bacc("TRN2", target_bir_lowering=False, num_devices=1)
    aps = {k: nc.dram_tensor(f"in_{k}", v.shape, mybir.dt.from_np(v.dtype), kind="ExternalInput").ap()
           for k, v in host.items()}
    aps["out"] = nc.dram_tensor("out_0", _OUT, mybir.dt.float32, kind="ExternalOutput").ap()
    audio_tower(nc, **aps)
    r = run_bass_kernel_spmd(nc, [{f"in_{k}": v for k, v in host.items()}], core_ids=[0])
    return r.results[0]["out_0"]
```

```python
from contextlib import ExitStack

import concourse.bass as bass
from concourse import mybir

B, T, D = 8, 375, 128
BN = 64
TP = T - 2
E, H = 8, 256
NJ = 3
P = T // NJ
ROWS = [len(range(j, TP, NJ)) for j in range(NJ)]
OFF = [sum(ROWS[:j]) for j in range(NJ)]
TE = TP + 1
HC = H // 128
NC = E * HC
KC = 72
EPS = 1e-5
SCALE = float(D) ** -0.5

LAG = {"xb": 0, "a1": 0, "a2": 0, "a3": 0, "a3b": 0,
       "a4": 1, "a5": 1, "a6": 1, "a6b": 1,
       "s3a": 2, "s3b": 2, "xnv": 2, "b1": 2, "b2": 2,
       "sc": 3, "pt": 3, "at": 3, "atb": 3,
       "h1": 4, "g1": 4, "g2": 4, "g3": 4, "g3b": 4, "g4": 4,
       "w1": 1, "w1lo": 2, "moe": 5, "yo": 6, "out": 6}
PE_ORDER = ["a1", 0, 1, 2, 3, "h1", "a4", "a2", 4, 5, "g1", "a5", 6, 7, "a3", "g2", "a6", 8, 9, 10, "sc", "b1", 11,
            12, "pt", 13, "b2", 14, 15, "at", "g4", "out", "flush"]
DVE_ORDER = [0, "a1", 1, 2, 3, "s3a", 4, "a2", 5, "h1", 6, "s3b", "a3", 7, 8, "g2", "a6", "sc", 9, "a3b", 10, "g3",
             "pt", 11, 12, "a6b", 13, "g3b", "b2", 14, "at", 15, "out", "atb"]
ACT_ORDER = [0, 1, "a1", 2, 3, "a4", "h1", "a2", 4, 5, "g1", "w1", 6, "a5", "yo", 7, "xnv", 8, 9, 10, "sc", "g2", 11,
             "b1", 12, "pt", 13, "g3", "b2", 14, 15, "flush", "g4"]
POOL_ORDER = [0, 1, 2, "xb", 3, 4, 5, "s3a", 6, 7, 8, "a6", "a3", 9, 10, 11, 12, 13, 14, "a3b", 15, "flush", "w1lo",
              "at"]
SP_ORDER = ["a6b", "out"]
STEPS = B + 6
LAG_HI, LAG_LO, LAG2 = 2, 3, 8
SC_BANK = [0, 1, 2]
PT_BANK = [1, 2, 0]


START = [0, 13, 26, 39, 52]
AT = {"xb": 6, "a1": 3, "a2": 5, "a3": 9, "a3b": 14, "a4": 18, "a5": 18, "a6": 21, "a6b": 24, "s3a": 28, "s3b": 31,
      "xnv": 32, "b1": 32, "b2": 35, "sc": 37, "pt": 40, "at": 44, "atb": 48, "h1": 50, "g1": 53, "g2": 54, "g3": 57,
      "g3b": 59, "g4": 63, "w1": 30, "w1lo": 52}


def pieces(order, t):
    for name in order:
        lag = LAG["moe" if name == "flush" or isinstance(name, int) else name]
        if 0 <= t - lag < B:
            yield name, t - lag


def schedule(order):
    names = [name for name in order if name in AT]
    fill = [(START[n] + AT[name], n, name) for name in names for n in range(LAG["moe"] - LAG[name])]
    yield from ((name, n) for _, n, name in sorted(fill))
    for t in range(LAG["moe"], STEPS + 1):
        yield from pieces(order, t)


def behind(n, k, lag):
    n, k = n + (k - lag) // NC, (k - lag) % NC
    return [(n, k)] if n >= 0 else []


def rest(n, lag):
    return [(n, k) for k in range(NC - lag, NC)] if n == B - 1 else []


def audio_tower(nc, x, xt, wc, wm, we, wf1, wf2, wq, wk, gw1, gw2, b64, b128, b_rows, gb2, we1, we2, be2, out):
    fp32, fp32r, u32 = mybir.dt.float32, mybir.dt.float32r, mybir.dt.uint32
    ALU, ACT, AX = mybir.AluOpType, mybir.ActivationFunctionType, mybir.AxisListType

    with ExitStack() as ctx:
        def sb(name, shape, dt=fp32):
            return ctx.enter_context(nc.sbuf_tensor(name, shape, dt))

        def sem(name):
            return ctx.enter_context(nc.semaphore(name))

        x_sb = sb("x_sb", [P, B, NJ * D])
        xt_sb = sb("xt_sb", [D, B, T])
        wc_sb = sb("wc_sb", [D, BN])
        wm_sb = sb("wm_sb", [BN, 3, BN])
        we_sb = sb("we_sb", [BN, D])
        wf1_sb = sb("wf1_sb", [D, BN])
        wf2_sb = sb("wf2_sb", [BN, D])
        wq_sb = sb("wq_sb", [D, D])
        wk_sb = sb("wk_sb", [D, D])
        gw1_sb = sb("gw1_sb", [D, BN])
        gw2_sb = sb("gw2_sb", [BN, E])
        bias64 = sb("bias64", [BN, 8])
        bias128 = sb("bias128", [D, 2 + NC])
        rows = sb("rows", [P, 6 * D])
        gb2_sb = sb("gb2_sb", [P, NJ * E])
        w1_sb = sb("w1_sb", [D, E, H])
        w1hi = sb("w1hi", [D, E, H], fp32r)
        w1lo = sb("w1lo", [D, E, H], fp32r)
        w2_sb = sb("w2_sb", [128, NC, D])
        w2hi = sb("w2hi", [128, NC, D], fp32r)
        w2lo = sb("w2lo", [128, NC, D], fp32r)
        be2_sb = sb("be2_sb", [KC, D])
        be2hi = sb("be2hi", [KC, D], fp32r)
        ident = sb("ident", [128, 128])
        sel32 = sb("sel32", [KC, E, D])
        sel = sb("sel", [KC, E, D], fp32r)
        iota_e = sb("iota_e", [P, NJ, E])
        mhalf = sb("mhalf", [P, NJ])

        th1, z1 = sb("th1", [BN, T]), sb("z1", [BN, T])
        th2, z2 = sb("th2", [BN, T]), sb("z2", [BN, T])
        hc1 = sb("hc1", [BN, T + 2])
        hc2 = sb("hc2", [BN, T])
        r1 = sb("r1", [P, NJ, D])
        n1 = sb("n1", [P, NJ, D])
        y = sb("y", [P, NJ, D])
        yb = sb("yb", [P, NJ, D])
        y_t = sb("y_t", [D, T])
        f1 = sb("f1", [BN, T])
        r2 = sb("r2", [P, NJ, D])
        n2 = sb("n2", [P, NJ, D])
        y2 = sb("y2", [P, NJ, D])
        y2next = sb("y2next", [P, 2, D])
        m12 = sb("m12", [P, D])
        m01 = sb("m01", [P, D])
        h = sb("h", [P, 2, NJ * D])
        xn3 = sb("xn3", [P, NJ, D])
        xn3v = sb("xn3v", [P, 2, NJ * D])
        xn_t = sb("xn_t", [D, TP])
        q_t = sb("q_t", [D, TE])
        k_t = sb("k_t", [D, TP])
        nmax = sb("nmax", [P, NJ])
        prob = sb("prob", [P, NJ, TP])
        psum_row = sb("psum_row", [P, NJ])
        rinv = sb("rinv", [P, NJ])
        prob_t = sb("prob_t", [P, NJ, TE])
        h2 = sb("h2", [P, 4, NJ * D])
        xn4 = sb("xn4", [P, NJ, D])
        x32 = sb("x32", [D, TP])
        xhi = sb("xhi", [D, 2, TE], fp32r)
        xlo = sb("xlo", [D, 2, TE], fp32r)
        gh_t = sb("gh_t", [BN, TE])
        lg = sb("lg", [P, NJ, E])
        lmax = sb("lmax", [P, NJ])
        le = sb("le", [P, NJ, E])
        ge = sb("ge", [P, NJ, E])
        gsum = sb("gsum", [P, NJ])
        grec = sb("grec", [P, NJ])
        gp = sb("gp", [P, NJ, E])
        top = sb("top", [P, NJ, 8])
        topi = sb("topi", [P, NJ, 8], u32)
        topf = sb("topf", [P, NJ, 2])
        dd = sb("dd", [P, NJ])
        th3 = sb("th3", [P, NJ])
        w_top = sb("w_top", [P, 2, NJ])
        one1, one2 = sb("one1", [P, NJ, E]), sb("one2", [P, NJ, E])
        s1, s2 = sb("s1", [P, NJ, E]), sb("s2", [P, NJ, E])
        comb = sb("comb", [P, NJ, E])
        chi = sb("chi", [P, NJ, E], fp32r)
        c3 = sb("c3", [P, NJ, KC])
        c_t = sb("c_t", [KC, 2, TE], fp32r)
        g_sb = [sb(f"g_sb{i}", [128, TP]) for i in range(4)]
        NG = 8
        gs_sb = [sb(f"gs_sb{i}", [128, TP]) for i in range(NG)]
        gs_hi = sb("gs_hi", [128, NG, TE], fp32r)
        gs_lo = sb("gs_lo", [128, NG, TE], fp32r)
        yo = sb("yo", [D, TE])
        ob = sb("ob", [P, NJ * D])
        stat = [sb(f"stat{i}", [P, NJ, 6]) for i in range(4)]
        mv = [sb(f"mv{i}", [P, NJ, 2]) for i in range(4)]
        ve = [sb(f"ve{i}", [P, NJ]) for i in range(4)]
        rstd = [sb(f"rstd{i}", [P, NJ]) for i in range(4)]

        def bank(name):
            return ctx.enter_context(nc.psum_tensor(name, [128, 512], fp32))

        F = [bank(f"F{i}") for i in range(3)]
        PH = [bank(f"PH{i}") for i in range(2)]
        CB = [bank(f"CB{i}") for i in range(2)]
        PY = bank("PY")

        names = """rows wearly wmid wlate xb ident init init2 wsplit w2split
            h1 x32 xs g1 gh g2 le ge g3 dd th3 c3 g4 ct
            a1 z1 hc1 a2 z2 hc2 a3 y yb a4 yt a5 f1 a6 y2 shift xn3 xnv b1 xnt qp kp q k
            sc nmax prob pt pta ptd at xn4 cb l1 gl gs l2 yo ot ob out r1 r2 h2 lg be2 one hi lo dve act""".split()
        S = {n: sem("s_" + n) for n in names}
        s_x = [sem(f"s_x{b}") for b in range(B)]
        s_xt = [sem(f"s_xt{b}") for b in range(B)]
        s_ve = [sem(f"s_ve{i}") for i in range(4)]
        s_rstd = [sem(f"s_rstd{i}") for i in range(4)]

        def wait(eng, name, value):
            if value > 0:
                eng.wait_ge(S[name], value)

        block = ctx.enter_context(nc.Block())

        @block.sync
        def _(sp):
            sp.dma_start(wc_sb[:], wc).then_inc(S["wearly"], 16)
            sp.dma_start(wm_sb[:], wm).then_inc(S["wearly"], 16)
            sp.dma_start(we_sb[:], we).then_inc(S["wearly"], 16)
            for b in range(B):
                sp.dma_start(xt_sb[:, b, :], xt[:, b, :]).then_inc(s_xt[b], 16)
                sp.dma_start(x_sb[:, b, :], x[b].rearrange("(p j) d -> p (j d)", j=NJ)).then_inc(s_x[b], 16)
                if b == 0:
                    sp.dma_start(rows[:], b_rows.broadcast_to([P, 6 * D])).then_inc(S["rows"], 16)
                    for dst, src in ((wf1_sb, wf1), (wf2_sb, wf2), (bias128, b128), (wq_sb, wq), (wk_sb, wk),
                                     (gw1_sb, gw1), (gw2_sb, gw2)):
                        sp.dma_start(dst[:], src).then_inc(S["wmid"], 16)
                    sp.dma_start(gb2_sb[:], gb2.broadcast_to([P, NJ * E])).then_inc(S["wmid"], 16)
            sp.dma_start(w1_sb[:], we1.rearrange("e d h -> d e h")).then_inc(S["wlate"], 16)
            sp.dma_start(w2_sb[:], we2.rearrange("e (c p) d -> p (e c) d", p=128)).then_inc(S["wlate"], 16)
            for name, n in schedule(SP_ORDER):
                if name == "a6b":
                    wait(sp, "y2", n + 1)
                    sp.dma_start(y2next[0:P - 1, :, :], y2[1:P, 0:2, :]).then_inc(S["shift"], 16)
                if name == "out":
                    wait(sp, "ob", n + 1)
                    sp.dma_start(out[n, 0:TP - 1, :].rearrange("(p j) d -> p (j d)", j=NJ),
                                 ob[0:P - 1, :]).then_inc(S["out"], 16)
                    sp.dma_start(out[n, TP - 1:TP, :], ob[P - 1:P, 0:D]).then_inc(S["out"], 16)
            sp.wait_ge(S["out"], 32 * B)

        def pool_piece(pool, name, n):
            if isinstance(name, int) or name == "flush":
                for m, k in rest(n, LAG_LO) if name == "flush" else behind(n, name, LAG_LO):
                    wait(pool, "hi", NC * m + k + 1)
                    pool.tensor_tensor(gs_lo[:, k % NG, 0:TP], gs_sb[k % NG][:],
                                       gs_hi[:, k % NG, 0:TP].bitcast(fp32), ALU.subtract).then_inc(S["lo"], 1)
            ln = {"a3": 0, "a6": 1, "s3a": 2, "at": 3}.get(name)
            if ln is not None:
                pool.wait_ge(s_ve[ln], n + 1)
                pool.tensor_tensor(rstd[ln][:], ve[ln][:], mhalf[:], ALU.pow).then_inc(s_rstd[ln], 1)
            if name == "w1lo" and n == 0:
                pool.wait_ge(S["wsplit"], 1)
                pool.tensor_tensor(w1lo[:], w1_sb[:], w1hi[:].bitcast(fp32), ALU.subtract).then_inc(S["wsplit"], 1)
                pool.wait_ge(S["w2split"], 1)
                pool.tensor_tensor(w2lo[:], w2_sb[:], w2hi[:].bitcast(fp32), ALU.subtract).then_inc(S["w2split"], 1)
            if name == "xb":
                pool.wait_ge(s_x[n], 16)
                v = x_sb[:, n, :].rearrange("p (j d) -> p j d", j=NJ)
                pool.tensor_tensor(v, v, rows[:, 0:D].unsqueeze(1).broadcast_to([P, NJ, D]), ALU.add)\
                    .then_inc(S["xb"], 1)
            if name == "a3b":
                wait(pool, "y", n + 1)
                pool.tensor_tensor(yb[:], y[:], rows[:, 3 * D:4 * D].unsqueeze(1).broadcast_to([P, NJ, D]), ALU.add)\
                    .then_inc(S["yb"], 1)

        @block.gpsimd
        def _(pool):
            pool.memset(ident[:], 0.0).then_inc(S["ident"], 1)
            pool.memset(sel32[:], 0.0).then_inc(S["ident"], 1)
            pool.wait_ge(S["ident"], 2)
            pool.affine_select(out=ident[:], in_=ident[:], compare_op=ALU.not_equal, fill=1.0, base=0,
                               pattern=[[-1, 128]], channel_multiplier=1).then_inc(S["ident"], 1)
            for i, r in enumerate((0, 32)):
                pool.wait_ge(S["ident"], 3 + i)
                v = sel32[r:r + E, :, :]
                pool.affine_select(out=v, in_=v, compare_op=ALU.not_equal, fill=1.0, base=0,
                                   pattern=[[-1, E], [0, D]], channel_multiplier=1).then_inc(S["ident"], 1)
            pool.wait_ge(S["ident"], 5)
            pool.iota(iota_e[:], [[0, NJ], [1, E]], base=0, channel_multiplier=0,
                      allow_small_or_imprecise_dtypes=True).then_inc(S["init"], 1)
            pool.memset(mhalf[:], -0.5).then_inc(S["init"], 1)
            for v in (hc1[:, 0:1], hc1[:, T + 1:T + 2], q_t[:, TP:TE], prob_t[:, :, TP:TE], gh_t[:, TP:TE],
                      yo[:, TP:TE], y2next[:], c3[:], be2_sb[:]):
                pool.memset(v, 0.0).then_inc(S["init"], 1)
            for v in (xhi[:, :, TP:TE], xlo[:, :, TP:TE], c_t[:, :, TP:TE], gs_hi[:, :, TP:TE], gs_lo[:, :, TP:TE]):
                pool.memset(v.bitcast(fp32), 0.0).then_inc(S["init"], 1)
            pool.wait_ge(S["rows"], 16)
            for name, n in schedule(POOL_ORDER):
                pool_piece(pool, name, n)


        @block.scalar
        def _(act):
            act.dma_start(bias64[:, 0:4], b64).then_inc(S["wearly"], 16)
            act.wait_ge(S["wearly"], 16 * 4)
            act.activation(bias64[:, 4:6], bias64[:, 0:2], ACT.Copy, scale=0.5).then_inc(S["act"], 1)
            act.wait_ge(S["act"], 1)

            for name, n in schedule(ACT_ORDER):
                if name == "a1":
                    wait(act, "a1", n + 1)
                    wait(act, "hc1", n)
                    act.activation(th1[:], F[2][0:BN, 0:T], ACT.Tanh, bias=bias64[:, 4:5], scale=0.5)
                    act.activation(z1[:], F[2][0:BN, 0:T], ACT.Identity, bias=bias64[:, 4:5], scale=0.5)\
                        .then_inc(S["z1"], 1)
                if name == "a2":
                    wait(act, "a2", n + 1)
                    wait(act, "hc2", n)
                    act.activation(th2[:], F[0][0:BN, 0:T], ACT.Tanh, bias=bias64[:, 5:6], scale=0.5)
                    act.activation(z2[:], F[0][0:BN, 0:T], ACT.Identity, bias=bias64[:, 5:6], scale=0.5)\
                        .then_inc(S["z2"], 1)
                if name == "a4":
                    wait(act, "a4", n + 1)
                    if n == 0:
                        act.wait_ge(S["wmid"], 16 * 8)
                    act.activation(y_t[:], F[2][:, 0:T], ACT.Copy).then_inc(S["yt"], 1)
                if name == "a5":
                    wait(act, "a5", n + 1)
                    act.activation(f1[:], F[2][0:BN, 0:T], ACT.Gelu, bias=bias64[:, 2:3]).then_inc(S["f1"], 1)
                if name == "w1" and n == 0:
                    act.wait_ge(S["init"], 16)
                    for r in (0, 32, 64):
                        act.dma_start(be2_sb[r:r + E, :], be2).then_inc(S["be2"], 16)
                    act.wait_ge(S["wlate"], 16 * 2)
                    act.activation(w1hi[:], w1_sb[:], ACT.Copy).then_inc(S["wsplit"], 1)
                    act.activation(w2hi[:], w2_sb[:], ACT.Copy).then_inc(S["w2split"], 1)
                if name == "xnv":
                    wait(act, "xn3", n + 1)
                    wait(act, "at", n - 1)
                    act.activation(xn3v[:, n % 2, :], xn3[:].rearrange("p j d -> p (j d)"), ACT.Copy)\
                        .then_inc(S["xnv"], 1)
                if name == "b1":
                    wait(act, "b1", n + 1)
                    act.activation(xn_t[:], F[0][:, 0:TP], ACT.Copy).then_inc(S["xnt"], 1)
                if name == "b2":
                    wait(act, "kp", n + 1)
                    act.activation(k_t[:], F[2][:, 0:TP], ACT.Identity, bias=bias128[:, 1:2])\
                        .then_inc(S["k"], 1)
                if name == "sc":
                    for j in range(NJ):
                        wait(act, "nmax", NJ * n + j + 1)
                        act.activation(prob[:, j, :], F[SC_BANK[j]][0:P, 0:TP], ACT.Exp, bias=nmax[:, j:j + 1],
                                       accum_out=psum_row[:, j:j + 1]).then_inc(S["prob"], 1)
                if name == "g2":
                    wait(act, "le", n + 1)
                    act.activation(ge[:], le[:], ACT.Exp).then_inc(S["ge"], 1)
                if name == "pt":
                    for c in (0, 2):
                        wait(act, "pt", NJ * n + c + 1)
                        act.activation(prob_t[0:ROWS[c], c, 0:TP], F[PT_BANK[c]][0:ROWS[c], 0:TP], ACT.Copy)\
                            .then_inc(S["pta"], 1)
                if name == "h1":
                    wait(act, "h1", n + 1)
                    wait(act, "xs", n)
                    act.activation(x32[:], F[1][:, 0:TP], ACT.Copy).then_inc(S["x32"], 1)
                if name == "g1":
                    wait(act, "g1", n + 1)
                    act.activation(gh_t[:, 0:TP], F[1][0:BN, 0:TP], ACT.Relu, bias=bias64[:, 3:4])\
                        .then_inc(S["gh"], 1)
                if name == "g3":
                    wait(act, "dd", n + 1)
                    act.activation(th3[:], dd[:], ACT.Tanh, scale=0.5).then_inc(S["th3"], 1)
                if name == "g4":
                    wait(act, "g4", n + 1)
                    wait(act, "l1", NC * (n - 1))
                    act.activation(c_t[:, n % 2, 0:TP], F[2][0:KC, 0:TP], ACT.Copy).then_inc(S["ct"], 1)
                if isinstance(name, int):
                    k = name
                    wait(act, "l1", NC * n + k + 1)
                    wait(act, "gs", NC * n + k - 3)
                    act.activation(g_sb[k % 4][:], PH[k % 2][:, 0:TP], ACT.Gelu, bias=bias128[:, 2 + k:3 + k])\
                        .then_inc(S["gl"], 1)
                if isinstance(name, int) or name == "flush":
                    for m, k in rest(n, LAG_HI) if name == "flush" else behind(n, name, LAG_HI):
                        wait(act, "gs", NC * m + k + 1)
                        act.activation(gs_hi[:, k % NG, 0:TP], gs_sb[k % NG][:], ACT.Copy).then_inc(S["hi"], 1)
                if name == "yo":
                    wait(act, "l2", NC * (n + 1))
                    wait(act, "ot", n)
                    act.activation(yo[:, 0:TP], PY[:, 0:TP], ACT.Copy).then_inc(S["yo"], 1)

        @block.vector
        def _(dve):
            chain = [0]

            def link(ins):
                chain[0] += 1
                ins.then_inc(S["dve"], 1)
                dve.wait_ge(S["dve"], chain[0])

            def bc(ap):
                return ap.broadcast_to([P, NJ, E])

            def ln_stats(i, src):
                for j in range(NJ):
                    last = dve.bn_stats(stat[i][:, j, :], src[j])
                link(last)
                for j in range(NJ):
                    last = dve.bn_aggr(mv[i][:, j, :], stat[i][:, j, :])
                link(last)
                dve.tensor_scalar(ve[i][:], mv[i][:, :, 1], EPS, None, ALU.add).then_inc(s_ve[i], 1)

            def ln_apply(i, n, src, dst):
                dve.wait_ge(s_rstd[i], n + 1)
                for j in range(NJ):
                    last = dve.tensor_scalar(dst[j], src[j], mv[i][:, j, 0:1], rstd[i][:, j:j + 1],
                                             ALU.subtract, ALU.mult)
                return last

            def tiles(ap):
                return [ap[:, j, :] for j in range(NJ)]

            def flat_tiles(ap, n):
                return [ap[:, n, j * D:(j + 1) * D] for j in range(NJ)]

            def row(i):
                return rows[:, i * D:(i + 1) * D].unsqueeze(1).broadcast_to([P, NJ, D])

            dve.wait_ge(S["ident"], 5)
            dve.tensor_copy(sel[:], sel32[:]).then_inc(S["init2"], 1)
            for name, n in schedule(DVE_ORDER):
                if name == "a1":
                    wait(dve, "z1", n + 1)
                    if n == 0:
                        dve.wait_ge(S["init"], 16)
                    dve.scalar_tensor_tensor(hc1[:, 1:T + 1], th1[:], 1.0, z1[:], ALU.add, ALU.mult)\
                        .then_inc(S["hc1"], 1)
                if name == "a2":
                    wait(dve, "z2", n + 1)
                    dve.scalar_tensor_tensor(hc2[:], th2[:], 1.0, z2[:], ALU.add, ALU.mult)\
                        .then_inc(S["hc2"], 1)
                if name == "a3":
                    wait(dve, "a3", n + 1)
                    wait(dve, "xb", n + 1)
                    dve.tensor_tensor(r1[:].rearrange("p j d -> p (j d)"), F[0][0:P, 0:NJ * D],
                                      x_sb[:, n, :], ALU.add).then_inc(S["r1"], 1)
                    wait(dve, "r1", n + 1)
                    ln_stats(0, tiles(r1))
                if name == "a3b":
                    link(ln_apply(0, n, tiles(r1), tiles(n1)))
                    link(dve.tensor_tensor(n1[:], n1[:], row(1), ALU.mult))
                    wait(dve, "a4", n)
                    wait(dve, "yb", n)
                    dve.tensor_tensor(y[:], n1[:], row(2), ALU.add).then_inc(S["y"], 1)
                if name == "a6":
                    wait(dve, "a6", n + 1)
                    wait(dve, "yb", n + 1)
                    dve.tensor_tensor(r2[:].rearrange("p j d -> p (j d)"), F[2][0:P, 0:NJ * D],
                                      yb[:].rearrange("p j d -> p (j d)"), ALU.add).then_inc(S["r2"], 1)
                    wait(dve, "r2", n + 1)
                    ln_stats(1, tiles(r2))
                if name == "a6b":
                    link(ln_apply(1, n, tiles(r2), tiles(n2)))
                    link(dve.tensor_tensor(n2[:], n2[:], row(4), ALU.mult))
                    dve.tensor_tensor(y2[:], n2[:], row(5), ALU.add).then_inc(S["y2"], 1)
                if name == "s3a" and n == 0:
                    dve.wait_ge(S["be2"], 16 * 3)
                    link(dve.tensor_copy(be2hi[:], be2_sb[:]))
                    link(dve.tensor_tensor(be2_sb[64:KC, :], be2_sb[64:KC, :], be2hi[64:KC, :].bitcast(fp32), ALU.subtract))
                    dve.tensor_copy(be2hi[64:KC, :], be2_sb[64:KC, :]).then_inc(S["init2"], 1)
                if name == "s3a":
                    wait(dve, "y2", n + 1)
                    wait(dve, "shift", 16 * (n + 1))
                    hn = flat_tiles(h, n % 2)
                    dve.tensor_tensor(m12[:], y2[:, 1, :], y2[:, 2, :], ALU.max)
                    link(dve.tensor_tensor(m01[:], y2next[:, 0, :], y2next[:, 1, :], ALU.max))
                    dve.tensor_tensor(hn[0], y2[:, 0, :], m12[:], ALU.max)
                    dve.tensor_tensor(hn[1], m12[:], y2next[:, 0, :], ALU.max)
                    link(dve.tensor_tensor(hn[2], y2[:, 2, :], m01[:], ALU.max))
                    ln_stats(2, hn)
                if name == "s3b":
                    wait(dve, "b1", n)
                    wait(dve, "xnv", n)
                    ln_apply(2, n, flat_tiles(h, n % 2), tiles(xn3)).then_inc(S["xn3"], 1)
                if name == "b2":
                    wait(dve, "qp", n + 1)
                    dve.tensor_scalar(q_t[:, 0:TP], F[1][:, 0:TP], bias128[:, 0:1], SCALE, ALU.add, ALU.mult)\
                        .then_inc(S["q"], 1)
                if name == "sc":
                    for j in range(NJ):
                        wait(dve, "sc", NJ * n + j + 1)
                        dve.tensor_reduce(nmax[:, j:j + 1], F[SC_BANK[j]][0:P, 0:TP], AX.X, ALU.max, negate=True)\
                            .then_inc(S["nmax"], 1)
                if name == "pt":
                    wait(dve, "pt", NJ * n + 2)
                    dve.tensor_copy(prob_t[0:ROWS[1], 1, 0:TP], F[PT_BANK[1]][0:ROWS[1], 0:TP]).then_inc(S["ptd"], 1)
                if name == "at":
                    wait(dve, "prob", NJ * (n + 1))
                    link(dve.reciprocal(rinv[:], psum_row[:]))
                    wait(dve, "at", n + 1)
                    for j in range(NJ):
                        last = dve.scalar_tensor_tensor(flat_tiles(h2, n % 4)[j], F[0][0:P, j * D:(j + 1) * D],
                                                        rinv[:, j:j + 1], flat_tiles(h, n % 2)[j], ALU.mult, ALU.add)
                    last.then_inc(S["h2"], 1)
                    wait(dve, "h2", n + 1)
                    ln_stats(3, flat_tiles(h2, n % 4))
                if name == "atb":
                    wait(dve, "h1", n)
                    ln_apply(3, n, flat_tiles(h2, n % 4), tiles(xn4)).then_inc(S["xn4"], 1)
                if name == "h1":
                    wait(dve, "x32", n + 1)
                    wait(dve, "l1", NC * (n - 1))
                    link(dve.tensor_copy(xhi[:, n % 2, 0:TP], x32[:]))
                    dve.tensor_tensor(xlo[:, n % 2, 0:TP], x32[:], xhi[:, n % 2, 0:TP].bitcast(fp32), ALU.subtract)\
                        .then_inc(S["xs"], 1)
                if name == "g2":
                    wait(dve, "g2", n + 1)
                    dve.tensor_tensor(lg[:], F[1][0:P, 0:NJ * E].rearrange("p (j e) -> p j e", j=NJ),
                                      gb2_sb[:].rearrange("p (j e) -> p j e", j=NJ), ALU.add).then_inc(S["lg"], 1)
                    wait(dve, "lg", n + 1)
                    link(dve.tensor_reduce(lmax[:], lg[:], AX.X, ALU.max))
                    dve.tensor_tensor(le[:], lg[:], bc(lmax[:].unsqueeze(2)), ALU.subtract).then_inc(S["le"], 1)
                if name == "g3":
                    wait(dve, "ge", n + 1)
                    link(dve.tensor_reduce(gsum[:], ge[:], AX.X, ALU.add))
                    link(dve.reciprocal(grec[:], gsum[:]))
                    link(dve.tensor_tensor(gp[:], ge[:], bc(grec[:].unsqueeze(2)), ALU.mult))
                    for j in range(NJ):
                        last = dve.max(top[:, j, :], gp[:, j, :])
                    link(last)
                    dve.tensor_tensor(dd[:], top[:, :, 1], top[:, :, 0], ALU.subtract).then_inc(S["dd"], 1)
                    for j in range(NJ):
                        last = dve.max_index(topi[:, j, :], top[:, j, :], gp[:, j, :])
                    link(last)
                    link(dve.tensor_copy(topf[:], topi[:, :, 0:2]))
                    dve.tensor_tensor(one1[:], iota_e[:], bc(topf[:, :, 0:1]), ALU.is_equal)
                    last = dve.tensor_tensor(one2[:], iota_e[:], bc(topf[:, :, 1:2]), ALU.is_equal)
                    last.then_inc(S["one"], 1)
                if name == "g3b":
                    wait(dve, "th3", n + 1)
                    wait(dve, "one", n + 1)
                    dve.tensor_scalar(w_top[:, 0, :], th3[:], -0.5, 0.5, ALU.mult, ALU.add)
                    link(dve.tensor_scalar(w_top[:, 1, :], th3[:], 0.5, 0.5, ALU.mult, ALU.add))
                    dve.tensor_tensor(s1[:], one1[:], bc(w_top[:, 0, :].unsqueeze(2)), ALU.mult)
                    link(dve.tensor_tensor(s2[:], one2[:], bc(w_top[:, 1, :].unsqueeze(2)), ALU.mult))
                    link(dve.tensor_tensor(comb[:], s1[:], s2[:], ALU.add))
                    link(dve.tensor_copy(chi[:], comb[:]))
                    wait(dve, "g4", n)
                    dve.tensor_copy(c3[:, :, 0:E], chi[:].bitcast(fp32))
                    dve.tensor_copy(c3[:, :, 64:64 + E], chi[:].bitcast(fp32))
                    dve.tensor_tensor(c3[:, :, 32:32 + E], comb[:], chi[:].bitcast(fp32), ALU.subtract)\
                        .then_inc(S["c3"], 1)
                if isinstance(name, int):
                    k = name
                    wait(dve, "gl", NC * n + k + 1)
                    wait(dve, "cb", E * n + k // HC + 1)
                    wait(dve, "l2", NC * n + k + 1 - NG)
                    dve.tensor_tensor(gs_sb[k % NG][:], g_sb[k % 4][:], CB[k // HC % 2][:, 0:TP], ALU.mult)\
                        .then_inc(S["gs"], 1)
                if name == "out":
                    wait(dve, "ot", n + 1)
                    wait(dve, "out", 32 * n)
                    dve.tensor_tensor(ob[:], F[1][0:P, 0:NJ * D], h2[:, n % 4, :], ALU.add).then_inc(S["ob"], 1)

        @block.tensor
        def _(pe):
            reader = [None] * 3

            def claim(f, name, value):
                if reader[f]:
                    wait(pe, *reader[f])
                reader[f] = (name, value)
                return F[f]

            def transposes(dst, src, rows_of, off, width=D):
                for j in range(NJ):
                    last = pe.transpose(dst[0:width, off[j]:off[j] + rows_of[j]], src[0:rows_of[j], j, 0:width],
                                        ident[0:rows_of[j], 0:rows_of[j]])
                return last

            def second_layer(n, k):
                if (n, k) == (0, 0):
                    pe.wait_ge(S["w2split"], 2)
                wait(pe, "lo", NC * n + k + 1)
                py = PY[:, 0:TE]
                pe.matmul(py, w2hi[:, k, :], gs_hi[:, k % NG, :], start=False, stop=False)
                pe.matmul(py, w2hi[:, k, :], gs_lo[:, k % NG, :], start=False, stop=False)
                pe.matmul(py, w2lo[:, k, :], gs_hi[:, k % NG, :], start=False, stop=(k == NC - 1))\
                    .then_inc(S["l2"], 1)

            pe.wait_ge(S["ident"], 5)
            pe.wait_ge(S["wearly"], 16 * 4)
            for name, n in schedule(PE_ORDER):
                if name == "a1":
                    pe.wait_ge(s_xt[n], 16)
                    f = claim(2, "z1", n + 1)
                    pe.matmul(f[0:BN, 0:T], wc_sb[:], xt_sb[:, n, :], start=True, stop=True).then_inc(S["a1"], 1)
                if name == "a2":
                    wait(pe, "hc1", n + 1)
                    f = claim(0, "z2", n + 1)
                    for k in range(3):
                        last = pe.matmul(f[0:BN, 0:T], wm_sb[:, k, :], hc1[:, k:k + T],
                                         start=(k == 0), stop=(k == 2))
                    last.then_inc(S["a2"], 1)
                if name == "a3":
                    wait(pe, "hc2", n + 1)
                    f = claim(0, "r1", n + 1)
                    for j in range(NJ):
                        last = pe.matmul(f[0:P, j * D:(j + 1) * D], hc2[:, j:T:NJ], we_sb[:],
                                         start=True, stop=True)
                    last.then_inc(S["a3"], 1)
                if name == "a4":
                    wait(pe, "y", n + 1)
                    f = claim(2, "yt", n + 1)
                    transposes(f, y, [P] * NJ, [P * j for j in range(NJ)]).then_inc(S["a4"], 1)
                if name == "a5":
                    wait(pe, "yt", n + 1)
                    if n == 0:
                        pe.wait_ge(S["wmid"], 16 * 8)
                    f = claim(2, "f1", n + 1)
                    pe.matmul(f[0:BN, 0:T], wf1_sb[:], y_t[:], start=True, stop=True).then_inc(S["a5"], 1)
                if name == "a6":
                    wait(pe, "f1", n + 1)
                    f = claim(2, "r2", n + 1)
                    for j in range(NJ):
                        last = pe.matmul(f[0:P, j * D:(j + 1) * D], f1[:, j * P:(j + 1) * P], wf2_sb[:],
                                         start=True, stop=True)
                    last.then_inc(S["a6"], 1)
                if name == "b1":
                    wait(pe, "xn3", n + 1)
                    f = claim(0, "xnt", n + 1)
                    transposes(f, xn3, ROWS, OFF).then_inc(S["b1"], 1)
                if name == "b2":
                    wait(pe, "xnt", n + 1)
                    f = claim(1, "q", n + 1)
                    pe.matmul(f[:, 0:TP], wq_sb[:], xn_t[:], start=True, stop=True).then_inc(S["qp"], 1)
                    f = claim(2, "k", n + 1)
                    pe.matmul(f[:, 0:TP], wk_sb[:], xn_t[:], start=True, stop=True).then_inc(S["kp"], 1)
                if name == "sc":
                    wait(pe, "q", n + 1)
                    wait(pe, "k", n + 1)
                    for j in range(NJ):
                        f = claim(SC_BANK[j], "prob", NJ * n + j + 1)
                        pe.matmul(f[0:P, 0:TP], q_t[:, OFF[j]:OFF[j] + P], k_t[:], start=True, stop=True)\
                            .then_inc(S["sc"], 1)
                if name == "pt":
                    wait(pe, "prob", NJ * (n + 1))
                    for c in range(NJ):
                        f = claim(PT_BANK[c], *(("ptd", n + 1) if c == 1 else ("pta", 2 * n + c // 2 + 1)))
                        for j in range(NJ):
                            last = pe.transpose(f[0:ROWS[c], OFF[j]:OFF[j] + ROWS[j]],
                                                prob[0:ROWS[j], j, OFF[c]:OFF[c] + ROWS[c]],
                                                ident[0:ROWS[j], 0:ROWS[j]])
                        last.then_inc(S["pt"], 1)
                if name == "at":
                    wait(pe, "pta", 2 * (n + 1))
                    wait(pe, "ptd", n + 1)
                    wait(pe, "xnv", n + 1)
                    f = claim(0, "h2", n + 1)
                    for j in range(NJ):
                        for c in range(NJ):
                            last = pe.matmul(f[0:P, j * D:(j + 1) * D],
                                             prob_t[0:ROWS[c], c, OFF[j]:OFF[j] + P],
                                             xn3v[0:ROWS[c], n % 2, c * D:(c + 1) * D],
                                             start=(c == 0), stop=(c == NJ - 1))
                    last.then_inc(S["at"], 1)
                if name == "h1":
                    wait(pe, "xn4", n + 1)
                    f = claim(1, "x32", n + 1)
                    transposes(f, xn4, ROWS, OFF).then_inc(S["h1"], 1)
                if name == "g1":
                    wait(pe, "x32", n + 1)
                    f = claim(1, "gh", n + 1)
                    pe.matmul(f[0:BN, 0:TP], gw1_sb[:], x32[:], start=True, stop=True).then_inc(S["g1"], 1)
                if name == "g2":
                    wait(pe, "gh", n + 1)
                    f = claim(1, "lg", n + 1)
                    for j in range(NJ):
                        last = pe.matmul(f[0:P, j * E:(j + 1) * E], gh_t[:, OFF[j]:OFF[j] + P], gw2_sb[:],
                                         start=True, stop=True)
                    last.then_inc(S["g2"], 1)
                if name == "g4":
                    wait(pe, "c3", n + 1)
                    f = claim(2, "ct", n + 1)
                    transposes(f, c3, ROWS, OFF, KC).then_inc(S["g4"], 1)
                if isinstance(name, int):
                    k, e = name, name // HC
                    if k == 0:
                        wait(pe, "ct", n + 1)
                        wait(pe, "xs", n + 1)
                        if n == 0:
                            pe.wait_ge(S["wsplit"], 2)
                            pe.wait_ge(S["init2"], 2)
                    if k % HC == 0:
                        wait(pe, "gs", NC * n + HC * (e - 1))
                        pe.matmul(CB[e % 2][:, 0:TE], sel[:, e, :], c_t[:, n % 2, :], start=True, stop=True)\
                            .then_inc(S["cb"], 1)
                    wait(pe, "gl", NC * n + k - 1)
                    c = k % HC * 128
                    ph = PH[k % 2][:, 0:TE]
                    pe.matmul(ph, w1hi[:, e, c:c + 128], xhi[:, n % 2, :], start=True, stop=False)
                    pe.matmul(ph, w1hi[:, e, c:c + 128], xlo[:, n % 2, :], start=False, stop=False)
                    pe.matmul(ph, w1lo[:, e, c:c + 128], xhi[:, n % 2, :], start=False, stop=True)\
                        .then_inc(S["l1"], 1)
                    if k == LAG2:
                        wait(pe, "yo", n)
                        pe.matmul(PY[:, 0:TE], be2hi[:], c_t[:, n % 2, :], start=True, stop=False)
                    for m, k2 in behind(n, k, LAG2):
                        second_layer(m, k2)
                if name == "flush":
                    for m, k2 in rest(n, LAG2):
                        second_layer(m, k2)
                if name == "out":
                    wait(pe, "yo", n + 1)
                    f = claim(1, "ob", n + 1)
                    for j in range(NJ):
                        last = pe.transpose(f[0:P, j * D:(j + 1) * D], yo[:, OFF[j]:OFF[j] + P], ident[:])
                    last.then_inc(S["ot"], 1)


_OUT = (B, TP, D)


def kernel(x, L0_tok_w_compress, L0_tok_b_compress, L0_tok_w_main, L0_tok_b_main, L0_tok_w_expand,
           L0_tok_b_expand, L0_tok_g_conv_norm, L0_tok_b_conv_norm, L0_tok_w_ff1, L0_tok_b_ff1, L0_tok_w_ff2,
           L0_tok_b_ff2, L0_tok_g_ff_norm, L0_tok_b_ff_norm, L0_attn_Wq, L0_attn_bq, L0_attn_Wk, L0_attn_bk,
           L0_ffn_gw1, L0_ffn_gb1, L0_ffn_gw2, L0_ffn_gb2, L0_ffn_we1, L0_ffn_be1, L0_ffn_we2, L0_ffn_be2):
    import numpy as np
    import concourse.bacc as bacc
    from concourse.bass_utils import run_bass_kernel_spmd

    def a(v, *order):
        v = np.asarray(v)
        return np.ascontiguousarray(v.transpose(order) if order else v)

    def cols(*vs):
        return np.ascontiguousarray(np.stack([np.asarray(v) for v in vs], axis=1))

    host = {
        "x": a(x), "xt": a(x, 2, 0, 1),
        "wc": a(L0_tok_w_compress, 1, 2, 0).reshape(D, BN), "wm": a(L0_tok_w_main, 1, 2, 0),
        "we": a(L0_tok_w_expand, 1, 2, 0).reshape(BN, D),
        "wf1": a(L0_tok_w_ff1, 1, 0), "wf2": a(L0_tok_w_ff2, 1, 0),
        "wq": a(L0_attn_Wq), "wk": a(L0_attn_Wk), "gw1": a(L0_ffn_gw1), "gw2": a(L0_ffn_gw2),
        "we1": a(L0_ffn_we1), "we2": a(L0_ffn_we2), "be2": a(L0_ffn_be2),
        "b64": cols(L0_tok_b_compress, L0_tok_b_main, L0_tok_b_ff1, L0_ffn_gb1),
        "b128": cols(L0_attn_bq, L0_attn_bk, *np.asarray(L0_ffn_be1).reshape(NC, 128)),
        "b_rows": np.concatenate([np.asarray(v) for v in (
            L0_tok_b_expand, L0_tok_g_conv_norm, L0_tok_b_conv_norm, L0_tok_b_ff2, L0_tok_g_ff_norm,
            L0_tok_b_ff_norm)]).reshape(1, 6 * D),
        "gb2": np.concatenate([np.asarray(L0_ffn_gb2)] * NJ).reshape(1, NJ * E),
    }
    nc = bacc.Bacc("TRN2", target_bir_lowering=False, num_devices=1)
    aps = {k: nc.dram_tensor(f"in_{k}", v.shape, mybir.dt.from_np(v.dtype), kind="ExternalInput").ap()
           for k, v in host.items()}
    aps["out"] = nc.dram_tensor("out_0", _OUT, mybir.dt.float32, kind="ExternalOutput").ap()
    audio_tower(nc, **aps)
    r = run_bass_kernel_spmd(nc, [{f"in_{k}": v for k, v in host.items()}], core_ids=[0])
    return r.results[0]["out_0"]
```
